# Optimizing a Trainium2 kernel written in Bass

```python
import numpy as np
import jax
import jax.numpy as jnp

def _softmax(x, axis=-1):
    return jax.nn.softmax(x, axis=axis)

def _gelu(x):
    return jax.nn.gelu(x, approximate=True)

def _silu(x):
    return jax.nn.silu(x)

def _sigmoid(x):
    return jax.nn.sigmoid(x)

def _layernorm(x, axis=-1, eps=1e-05):
    m = jnp.mean(x, axis=axis, keepdims=True)
    v = jnp.var(x, axis=axis, keepdims=True)
    return (x - m) / jnp.sqrt(v + eps)

def _scatter_add(tgt, idx, src, axis=0):
    return tgt.at[idx].add(src)

def _segment_sum(src, seg, n):
    return jax.ops.segment_sum(src, seg, n)
kernel_name = 'mk_seq_postln_d1_jaxref_r4_5de41b'

def setup_inputs(seed: int=0):
    np.random.seed(seed)
    _w = jnp.asarray

    def _L0_attn_setup():
        import jax, jax.numpy as jnp
        import numpy as np
        B, S, D, H = (2, 512, 256, 16)
        HD = D // H
        LN_EPS = 1e-05
        key = jax.random.key(seed)
        ks = jax.random.split(key, 8)
        inv = 1.0 / np.sqrt(D)
        return {'embedded': jax.random.normal(ks[0], (B, S, D), dtype=jnp.float32), 'Wq': jax.random.normal(ks[1], (D, D), dtype=jnp.float32) * inv, 'bq': jax.random.normal(ks[2], (D,), dtype=jnp.float32) * 0.01, 'Wk': jax.random.normal(ks[3], (D, D), dtype=jnp.float32) * inv, 'bk': jax.random.normal(ks[4], (D,), dtype=jnp.float32) * 0.01, 'Wv': jax.random.normal(ks[5], (D, D), dtype=jnp.float32) * inv, 'bv': jax.random.normal(ks[6], (D,), dtype=jnp.float32) * 0.01, 'gamma': jnp.ones((D,), dtype=jnp.float32), 'beta': jnp.zeros((D,), dtype=jnp.float32)}
    _L0_attn_in = _L0_attn_setup()

    def _L0_ffn_setup():
        import jax, jax.numpy as jnp
        import numpy as np
        D_IN, D_HID = (256, 1024)

        def _ternary(key, shape):
            return jax.random.randint(key, shape, -1, 2).astype(jnp.float32)

        def _tlin(x, w, s):
            return jnp.einsum('bsi,oi->bso', x, w) * s
        key = jax.random.key(seed)
        ks = jax.random.split(key, 12)
        inv = lambda fan: 1.0 / np.sqrt(fan).astype(np.float32)
        return {'x': jax.random.normal(ks[0], (4, 512, D_IN), dtype=jnp.float32), 'w1_w': _ternary(ks[1], (D_HID, D_IN)), 'w1_s': jax.random.uniform(ks[2], (D_HID,), dtype=jnp.float32) * inv(D_IN), 'w2_w': _ternary(ks[3], (D_HID, D_IN)), 'w2_s': jax.random.uniform(ks[4], (D_HID,), dtype=jnp.float32) * inv(D_IN), 'h1_w': _ternary(ks[5], (D_HID, D_HID)), 'h1_s': jax.random.uniform(ks[6], (D_HID,), dtype=jnp.float32) * inv(D_HID), 'h2_w': _ternary(ks[7], (D_HID, D_HID)), 'h2_s': jax.random.uniform(ks[8], (D_HID,), dtype=jnp.float32) * inv(D_HID), 'w3_w': _ternary(ks[9], (D_IN, D_HID)), 'w3_s': jax.random.uniform(ks[10], (D_IN,), dtype=jnp.float32) * inv(D_HID)}
    _L0_ffn_in = _L0_ffn_setup()
    _d = {'L0_attn_embedded': _L0_attn_in['embedded'], 'L0_attn_Wq': _L0_attn_in['Wq'], 'L0_attn_bq': _L0_attn_in['bq'], 'L0_attn_Wk': _L0_attn_in['Wk'], 'L0_attn_bk': _L0_attn_in['bk'], 'L0_attn_Wv': _L0_attn_in['Wv'], 'L0_attn_bv': _L0_attn_in['bv'], 'L0_attn_gamma': _L0_attn_in['gamma'], 'L0_attn_beta': _L0_attn_in['beta'], 'L0_ffn_w1_w': _L0_ffn_in['w1_w'], 'L0_ffn_w1_s': _L0_ffn_in['w1_s'], 'L0_ffn_w2_w': _L0_ffn_in['w2_w'], 'L0_ffn_w2_s': _L0_ffn_in['w2_s'], 'L0_ffn_h1_w': _L0_ffn_in['h1_w'], 'L0_ffn_h1_s': _L0_ffn_in['h1_s'], 'L0_ffn_h2_w': _L0_ffn_in['h2_w'], 'L0_ffn_h2_s': _L0_ffn_in['h2_s'], 'L0_ffn_w3_w': _L0_ffn_in['w3_w'], 'L0_ffn_w3_s': _L0_ffn_in['w3_s']}
    _x0 = _d['L0_attn_embedded']
    _d['L0_attn_embedded'] = jax.random.normal(jax.random.fold_in(jax.random.key(seed), 1), (8, 512, 256), dtype=_x0.dtype)
    del _x0
    return _d

def reference(L0_attn_embedded, L0_attn_Wq, L0_attn_bq, L0_attn_Wk, L0_attn_bk, L0_attn_Wv, L0_attn_bv, L0_attn_gamma, L0_attn_beta, L0_ffn_w1_w, L0_ffn_w1_s, L0_ffn_w2_w, L0_ffn_w2_s, L0_ffn_h1_w, L0_ffn_h1_s, L0_ffn_h2_w, L0_ffn_h2_s, L0_ffn_w3_w, L0_ffn_w3_s):

    def _L0_attn_ref(embedded, Wq, bq, Wk, bk, Wv, bv, gamma, beta):
        import jax, jax.numpy as jnp
        import numpy as np
        B, S, D, H = (2, 512, 256, 16)
        HD = D // H
        LN_EPS = 1e-05
        b, s, d = embedded.shape
        q = embedded @ Wq.T + bq
        k = embedded @ Wk.T + bk
        v = embedded @ Wv.T + bv
        q = q.reshape(b, s, H, HD).transpose(0, 2, 1, 3)
        k = k.reshape(b, s, H, HD).transpose(0, 2, 1, 3)
        v = v.reshape(b, s, H, HD).transpose(0, 2, 1, 3)
        qk = jnp.einsum('bhqd,bhkd->bhqk', q, k)
        qk = jnp.where(jnp.isnan(qk), -jnp.inf, qk)
        qk = qk / jnp.float32(np.sqrt(s))
        p = jax.nn.softmax(qk, axis=-1)
        p = jnp.where(jnp.isnan(p), 0.0, p)
        v = jnp.where(jnp.isnan(v), 0.0, v)
        mask = jnp.triu(jnp.ones((s, s), dtype=p.dtype), k=0)
        p = p * mask
        z = jnp.einsum('bhqk,bhkd->bhqd', p, v)
        z = z.reshape(b, s, d)
        x = embedded + z
        mu = jnp.mean(x, axis=-1, keepdims=True)
        var = jnp.mean(jnp.square(x - mu), axis=-1, keepdims=True)
        out = (x - mu) * jax.lax.rsqrt(var + LN_EPS) * gamma + beta
        return out

    def _L0_ffn_ref(x, w1_w, w1_s, w2_w, w2_s, h1_w, h1_s, h2_w, h2_s, w3_w, w3_s):
        import jax, jax.numpy as jnp
        import numpy as np
        D_IN, D_HID = (256, 1024)

        def _ternary(key, shape):
            return jax.random.randint(key, shape, -1, 2).astype(jnp.float32)

        def _tlin(x, w, s):
            return jnp.einsum('bsi,oi->bso', x, w) * s
        h = jax.nn.silu(_tlin(x, w1_w, w1_s)) * _tlin(x, w2_w, w2_s)
        h = jax.nn.gelu(_tlin(h, h1_w, h1_s), approximate=False)
        h = jax.nn.gelu(_tlin(h, h2_w, h2_s), approximate=False)
        return _tlin(h, w3_w, w3_s)
    x = L0_attn_embedded
    x = _layernorm(x + _L0_attn_ref(x, L0_attn_Wq, L0_attn_bq, L0_attn_Wk, L0_attn_bk, L0_attn_Wv, L0_attn_bv, L0_attn_gamma, L0_attn_beta), axis=-1)
    x = _layernorm(x + _L0_ffn_ref(x, L0_ffn_w1_w, L0_ffn_w1_s, L0_ffn_w2_w, L0_ffn_w2_s, L0_ffn_h1_w, L0_ffn_h1_s, L0_ffn_h2_w, L0_ffn_h2_s, L0_ffn_w3_w, L0_ffn_w3_s), axis=-1)
    return x

_drawn_inputs = setup_inputs


def setup_inputs(seed=0):
    import zlib

    import numpy as np

    out = dict(_drawn_inputs(seed))
    spreads = {'L0_attn_gamma': (1.0, 0.2), 'L0_attn_beta': (0.0, 0.1)}
    factors = {'L0_attn_Wq': 8.0,
     'L0_attn_bq': 8.0,
     'L0_attn_Wk': 8.0,
     'L0_attn_bk': 64.0,
     'L0_attn_Wv': 3.527,
     'L0_attn_bv': 25.341,
     'L0_ffn_w1_w': 8.0,
     'L0_ffn_w1_s': 8.0,
     'L0_ffn_w2_w': 8.0,
     'L0_ffn_w2_s': 8.0,
     'L0_ffn_h1_w': 8.0,
     'L0_ffn_h1_s': 8.0,
     'L0_ffn_h2_w': 8.0,
     'L0_ffn_h2_s': 8.0,
     'L0_ffn_w3_w': 8.0,
     'L0_ffn_w3_s': 8.0}
    for name, (base, spread) in spreads.items():
        noise = np.random.default_rng([zlib.crc32(name.encode()), seed]).standard_normal(out[name].shape)
        drawn = base * np.exp(spread * noise) if base else spread * noise
        out[name] = jnp.asarray(drawn.astype(out[name].dtype))
    for name, factor in factors.items():
        out[name] = (out[name] * factor).astype(out[name].dtype)
    return out
```

```python
from contextlib import ExitStack

import concourse.bass as bass
from concourse import mybir

F32 = mybir.dt.float32
F32R = mybir.dt.float32r
I32 = mybir.dt.int32
ALU = mybir.AluOpType
ACT = mybir.ActivationFunctionType
AX = mybir.AxisListType

P = 128
B, S, D = 8, 512, 256
H, HD = 16, 16
DH = 1024
QT = S // P
DT = D // P
HT = DH // P
QUAD = 4
NQUAD = H // QUAD
SPLIT = 4 * HD
ROWS = SPLIT + 2
VW = HD + 1
VX = 288
EPS = 1e-5
PIECE = 2048
SCALE = 1.0 / float(S) ** 0.5
RSQRT_SEED = float(0x5F3759DF)
NEWTON = 3
NORM_STEPS = 3 + 3 * NEWTON
STEPS = NQUAD * QT
RING = 4
LAG = 2
TURN_MAX_AT = 5
KB = 1024


def build_program(nc, x, xT, wqT, wkT, wvT, bqk, bv, gamma, beta, w1T, w2T, h1T, h2T, scales,
                  w3T, s3, ident, out):
    base = (nc.sbuf_base + 63) // 64 * 64
    top = [base]

    def place(name, shape, dt, at=None):
        size = 4
        for n in shape[1:]:
            size *= n
        where = top[0] if at is None else at
        if at is None:
            top[0] += (size + 31) // 32 * 32
        return nc.alloc_sbuf_tensor_at(name, shape, dt, offset=where)

    def both(name, shape, at=None):
        rounded = place(name, shape, F32R, at)
        return rounded, rounded[:].bitcast(F32)

    def raw_and_rounded(name, shape):
        where = top[0]
        return place(name, shape, F32R), place(name + "_raw", shape, F32, where)

    W1, W1f = raw_and_rounded("w1", [P, DT, DH])
    W2, W2f = raw_and_rounded("w2", [P, DT, DH])
    G1, G1f = raw_and_rounded("g1", [P, HT, DH])
    G2, G2f = raw_and_rounded("g2", [P, HT, DH])
    W3, W3f = raw_and_rounded("w3", [P, HT, D])
    WQ = place("wq", [P, DT, D], F32)
    WK = place("wk", [P, DT, D], F32)
    WV = place("wv", [P, DT, D], F32)

    A = top[0]
    hidA_hi, hidA_hif = both("hidA_hi", [P, HT, S])
    hidA_full = place("hidA_full", [P, HT, S], F32, top[0])
    hidA_lo, hidA_lof = both("hidA_lo", [P, HT, S])
    PT = place("probsT", [P, RING, QUAD, S], F32, A)
    QKf = place("qk_full", [P, 2 * DT, S], F32, A)
    QKhi, QKhi_f = both("qk_hi", [P, 2 * DT, S], A + 8 * KB)
    QKlo, QKlo_f = both("qk_lo", [P, 2 * DT, S], A + 16 * KB)
    Vt = place("v_biased", [P, QT, D], F32, A + 24 * KB)
    Vm = place("v_negative", [P, QT, D], F32, A + 28 * KB)
    C = top[0]
    hidC_hi, hidC_hif = both("hidC_hi", [P, HT, S])
    hidC_full = place("hidC_full", [P, HT, S], F32, top[0])
    hidC_lo, hidC_lof = both("hidC_lo", [P, HT, S])
    X2hi, X2hif = both("x2T_hi", [P, DT, S], C)
    X2lo, X2lof = both("x2T_lo", [P, DT, S], C + 4 * KB)
    SIL = place("gate", [P, 2, S], F32, C + 8 * KB)
    XT = place("xT_sb", [P, DT, S], F32, C + 12 * KB)
    PM = place("diag_probs", [P, 2, QUAD, P], F32, C + 16 * KB)
    ZB = place("z_blocks", [P, HD, 2 * HD], F32, C + 20 * KB)
    LOW = place("low_bits_piece", [P, PIECE], I32, C)
    Z = place("z", [P, QT, D], F32, C + 24 * KB)
    T1 = place("norm_tmp", [P, QT, D], F32, C + 28 * KB)

    ST, ST_f = both("stacks", [ROWS, 2, QUAD, 2, S])
    VXT = place("v_ones", [P, QT, VX], F32)
    X = place("x_tok", [P, QT, D], F32)
    OUT = place("out_tok", [P, QT, D], F32)
    GAM = place("gamma_b", [P, D], F32)
    BET = place("beta_b", [P, D], F32)
    BV = place("bv_b", [P, D], F32)
    S3 = place("s3_b", [P, D], F32)
    ID = place("ident_sb", [P, P], F32)
    MASK = place("mask", [P, P], F32)
    ONE = place("ones_col", [P, 32], F32)
    WB = place("w_chunk", [P, 2, S], F32)
    BQK = place("bqk", [P, 2 * DT], F32)
    SC = place("scales", [P, 4, HT], F32)
    NEGM = place("neg_max", [P, P], F32)
    MROW, MROW_f = both("max_rows", [H * QT, 2, P])
    REC = place("rec", [P, HD], F32)
    STAT = place("stats", [P, QT, 6], F32)
    MV = place("mean_var", [P, QT, 2], F32)
    NV = place("neg_half_var", [P, QT], F32)
    NI = place("seed_bits", [P, QT], I32)
    NY = place("rstd", [P, QT], F32)
    NY_i = NY[:].bitcast(I32)
    NT = place("newton_tmp", [P, QT], F32)
    BITS = place("low_bits", [P, 12], I32)
    BITS1 = place("low_bits_most", [P, 1], I32)
    BITF = place("low_bits_f", [P, 1], F32)
    ONESF = place("ones_f", [P, 1], F32)
    FLAG = place("inexact", [1, 1], I32)
    assert top[0] <= nc.sbuf_usable_end, top[0] - nc.sbuf_usable_end

    qk_rows = nc.dram_tensor("qk_rows", [4, D, 2, S], F32, kind="Internal").ap()
    max_rows = nc.dram_tensor("max_rows_d", [2, H * QT * P], F32, kind="Internal").ap()

    with ExitStack() as ctx:
        PS = ctx.enter_context(nc.psum_tensor("PS", [P, 8, 512], F32))

        def sem(name):
            return ctx.enter_context(nc.semaphore(name))

        consts_in, qkv_w_in = sem("consts_in"), sem("qkv_w_in")
        w_in = [sem(f"w_in{n}") for n in range(5)]
        xT_in, x_in = sem("xT_in"), sem("x_in")
        rows_stored, max_stored, out_stored = sem("rows_stored"), sem("max_stored"), sem("out_stored")
        stack_in = [sem("stack_in0"), sem("stack_in1")]
        chunk_in = [sem("chunk_in0"), sem("chunk_in1")]
        consts_set, bits_seen, w_rounded = sem("consts_set"), sem("bits_seen"), sem("w_rounded")
        bits_cut = sem("bits_cut")
        bits_f, bits_summed, flag_set = sem("bits_f"), sem("bits_summed"), sem("flag_set")
        masks_set = sem("masks_set")
        scored = sem("scored")
        maxed = sem("maxed")
        max_turned, max_hi_done, max_split = sem("max_turned"), sem("max_hi_done"), sem("max_split")
        scoredT = sem("scoredT")
        exp_done = sem("exp_done")
        probs_ready = sem("probs_ready")
        diag_ready = sem("diag_ready")
        pv_done = sem("pv_done")
        zT_taken = sem("zT_taken")
        rec_done, z_taken = sem("rec_done"), sem("z_taken")
        qk_proj, qk_biased, qk_hi_done, qk_split = sem("qk_proj"), sem("qk_biased"), sem("qk_hi_done"), sem("qk_split")
        v_proj, v_taken, v_step, v_ready = sem("v_proj"), sem("v_taken"), sem("v_step"), sem("v_ready")
        norm_step, last_step = sem("norm_step"), sem("last_step")
        x2_ready, x2_turned, x2_hi_done, x2_split = sem("x2_ready"), sem("x2_turned"), sem("x2_hi_done"), sem("x2_split")
        ffn1, gate_done, up_done = sem("ffn1"), sem("gate_done"), sem("up_done")
        ffn23, gelu_done = sem("ffn23"), sem("gelu_done")
        hi_done, lo_done = sem("hi_done"), sem("lo_done")
        y_done, y_taken, out_ready = sem("y_done"), sem("y_taken"), sem("out_ready")
        chunk_used = sem("chunk_used")
        block = ctx.enter_context(nc.Block())

        def per_batch(engine, body):
            body(0, True, False)
            with engine.Fori(1, B - 1) as b:
                body(b, False, False)
            body(B - 1, False, True)

        def after(engine, s, b, n, count):
            value = n * b + count
            if isinstance(value, int) and value <= 0:
                return
            engine.wait_ge(s, value)

        LOADS_S, LOADS_T = 16, 32
        IN_PER_BATCH = 2 * LOADS_S + 2 * LOADS_T

        def after_stack(engine, b, group, transposed):
            had = (2 * LOADS_S + (group // 2) * LOADS_T + LOADS_T) if transposed else (group // 2 + 1) * LOADS_S
            after(engine, stack_in[group % 2], b, IN_PER_BATCH, had)

        def heads_beside(layer, m):
            if layer == 2:
                return [m]
            return [HT + 2 * m, HT + 2 * m + 1] if m < 4 else []

        def bank1(m, which):
            return 4 + (2 * m + 2 + which) % 4

        def bank23(m):
            return 4 + (m + 2) % 4

        def bank_qk(n):
            return 4 + (n + 2) % 4

        CHUNKS = 2 * HT + 2 * 2 * HT + QT * 4

        PIECES = [(n, at) for n, size in enumerate((DT * DH, DT * DH, HT * DH, HT * DH, HT * D))
                  for at in range(0, size, PIECE)]
        N_CONSTS = 7
        @block.sync
        def _(sp):
            for w, src in ((WQ, wqT), (WK, wkT), (WV, wvT)):
                sp.dma_start(w[:], src.rearrange("(t p) m -> p t m", p=P)).then_inc(qkv_w_in, 16)
            sp.dma_start(XT[:], xT[0:D, :].rearrange("(t p) s -> p t s", p=P)).then_inc(xT_in, 16)
            sp.dma_start(BQK[:], bqk).then_inc(consts_in, 16)
            sp.dma_start(SC[:], scales.rearrange("p (n t) -> p n t", n=4)).then_inc(consts_in, 16)
            sp.dma_start(BV[:], bv.rearrange("(a d) -> a d", a=1).to_broadcast([P, D])).then_inc(consts_in, 16)
            sp.dma_start(ID[:], ident).then_inc(consts_in, 16)
            for t, src in ((GAM, gamma), (BET, beta), (S3, s3)):
                sp.dma_start(t[:], src.rearrange("(a d) -> a d", a=1).to_broadcast([P, D])).then_inc(consts_in, 16)

            def load_stacks(b, group, transposed):
                n, back = 2 * H, 2 * QUAD * (group - 1)
                if group >= 2:
                    after(sp, scoredT if transposed else scored, b, n, back)
                else:
                    after(sp, scored if transposed else scoredT, b, n, back + n - (0 if transposed else n))
                if group == 0 and not transposed:
                    after(sp, rows_stored, b, 8 * 16, 8 * 16)
                rows = qk_rows.rearrange("r (d h) a s -> (r d) h a s", d=HD)
                sp.dma_start(ST_f[0:SPLIT, group % 2, :, :, :],
                             rows[:, group * QUAD:(group + 1) * QUAD, :, :]).then_inc(stack_in[group % 2], 16)
                if transposed:
                    if group == 0:
                        after(sp, max_stored, b, 16, 16)
                    sp.dma_start(ST_f[SPLIT:ROWS, group % 2, :, 0, :],
                                 max_rows[:, group * QUAD * S:(group + 1) * QUAD * S].rearrange(
                                     "r (h s) -> r h s", h=QUAD)).then_inc(stack_in[group % 2], 16)

            def store_rows(b):
                after(sp, qk_split, b, 2 * DT, 2 * DT)
                for a, parts in enumerate(((QKhi_f, QKhi_f, QKlo_f, QKlo_f), (QKhi_f, QKlo_f, QKhi_f, QKlo_f))):
                    for r, part in enumerate(parts):
                        sp.dma_start(qk_rows[r, :, a, :].rearrange("(t p) s -> p t s", p=P),
                                     part[:, a * DT:(a + 1) * DT, :]).then_inc(rows_stored, 16)

            def chunks(b, first, count, source):
                for c in range(first, first + count):
                    after(sp, chunk_used, b, CHUNKS, c - 1)
                    src, shape = source(c - first)
                    sp.dma_start(WB[:, c % 2, 0:shape[0] * shape[1]].rearrange("p (k m) -> p k m", m=shape[1]),
                                 src).then_inc(chunk_in[c % 2], 16)

            def feed_forward(b, last, general):
                def hidden(src, m):
                    return lambda c: (src.rearrange("(k p) m -> p k m", p=P)[:, 4 * c:4 * c + 4, m * P:(m + 1) * P], (4, P))

                def head_group(g):
                    if not last:
                        load_stacks(b + 1, g, False)

                if not general:
                    if not last:
                        for g in range(NQUAD):
                            load_stacks(b + 1, g, False)
                    return
                head_group(0)
                head_group(1)
                c0 = 0
                for m in range(HT):
                    for w in (w1T, w2T):
                        chunks(b, c0, 1, lambda c: (w.rearrange("(k p) m -> p k m", p=P)[:, :, m * P:(m + 1) * P], (DT, P)))
                        c0 += 1
                for layer, w in ((2, h1T), (3, h2T)):
                    for m in range(HT):
                        if (layer, m) == (2, 4):
                            head_group(2)
                        if (layer, m) == (3, 0):
                            head_group(3)
                        chunks(b, c0, 2, hidden(w, m))
                        c0 += 2
                for t in range(QT):
                    chunks(b, c0, 4, lambda c: (w3T.rearrange("(k p) m -> p k m", p=P)[:, 2 * c:2 * c + 2, :], (2, D)))
                    c0 += 4

            store_rows(0)
            for g in range(NQUAD):
                load_stacks(0, g, False)
            after(sp, max_split, 0, 1, 1)
            sp.dma_start(max_rows.rearrange("r (q p) -> q r p", p=P), MROW_f).then_inc(max_stored, 16)
            inexact = []

            def body(b, first, last):
                here = b * S if isinstance(b, int) else sp.snap(b * S)
                before = (b - 1) * S if isinstance(b, int) else sp.snap((b - 1) * S)
                next_dims = (b + 1) * D if isinstance(b, int) else sp.snap((b + 1) * D)
                if not last:
                    if first:
                        sp.wait_ge(v_proj, QT)
                    else:
                        after(sp, y_done, b, QT, -QT + 1)
                    sp.dma_start(XT[:], xT[bass.ds(next_dims, D), :].rearrange("(t p) s -> p t s", p=P)).then_inc(xT_in, 16)
                for g in range(2):
                    load_stacks(b, g, True)
                after(sp, out_ready, b, QT, 0)
                if not first:
                    sp.dma_start(out[bass.ds(before, S), :].rearrange("(t p) d -> p t d", p=P), OUT[:]).then_inc(out_stored, 16)
                sp.dma_start(X[:], x[bass.ds(here, S), :].rearrange("(t p) d -> p t d", p=P)).then_inc(x_in, 16)
                for g in range(2, NQUAD):
                    load_stacks(b, g, True)
                if not last:
                    store_rows(b + 1)
                if first:
                    sp.wait_ge(flag_set, 1)
                    inexact.append(sp.value_load(FLAG[0:1, 0:1], min_val=0, max_val=1))
                with sp.If(inexact[0]):
                    feed_forward(b, last, True)
                if not last:
                    with sp.Else():
                        feed_forward(b, last, False)
                if not last:
                    after(sp, max_split, b, 1, 2)
                    sp.dma_start(max_rows.rearrange("r (q p) -> q r p", p=P), MROW_f).then_inc(max_stored, 16)

            per_batch(sp, body)
            sp.wait_ge(out_ready, QT * B)
            sp.dma_start(out[(B - 1) * S:B * S, :].rearrange("(t p) d -> p t d", p=P), OUT[:]).then_inc(out_stored, 16)
            sp.wait_ge(out_stored, 16 * B)
            sp.wait_ge(rows_stored, 8 * 16 * B)
            sp.wait_ge(max_stored, 16 * B)

        @block.gpsimd
        def _(pool):
            nc.gpsimd.memset(MASK[:], 1.0).then_inc(masks_set, 1)
            nc.gpsimd.memset(ONE[:], 0.0).then_inc(masks_set, 1)
            pool.wait_ge(masks_set, 2)
            nc.gpsimd.affine_select(out=MASK[:], in_=MASK[:], compare_op=ALU.is_ge, fill=0.0, base=0,
                                    pattern=[[-1, P]], channel_multiplier=1).then_inc(masks_set, 1)
            nc.gpsimd.memset(ONE[:, HD:HD + 1], 1.0).then_inc(masks_set, 1)

            def low_part(n_before, b, full, hi, lo, m):
                after(pool, hi_done, b, 3 * HT, n_before + m + 1)
                nc.gpsimd.tensor_tensor(lo[:, m, :], full[:, m, :], hi[:, m, :], ALU.subtract).then_inc(lo_done, 1)

            def masks(b, s):
                kt = s % QT
                after(pool, probs_ready, b, 2 * STEPS, 2 * s + 2)
                after(pool, pv_done, b, STEPS, s - 1)
                nc.gpsimd.tensor_tensor(PM[:, s % 2, :, :], PT[:, s % RING, :, kt * P:(kt + 1) * P],
                                        MASK[:].rearrange("p (a m) -> p a m", a=1).to_broadcast([P, QUAD, P]),
                                        ALU.mult).then_inc(diag_ready, 1)

            def body(b, first, last):
                for s in range(STEPS):
                    masks(b, s)
                if first:
                    for n, (w, wf) in enumerate(((W1, W1f), (W2, W2f), (G1, G1f), (G2, G2f), (W3, W3f))):
                        pool.wait_ge(bits_seen, sum(which <= n for which, _ in PIECES))
                        nc.gpsimd.tensor_copy(w[:], wf[:]).then_inc(w_rounded, 1)
                for m in range(HT):
                    low_part(0, b, hidA_full, hidA_hif, hidA_lo, m)
                for m in range(HT):
                    low_part(HT, b, hidC_full, hidC_hif, hidC_lo, m)
                for m in range(HT):
                    low_part(2 * HT, b, hidA_full, hidA_hif, hidA_lo, m)

            per_batch(pool, body)

        @block.scalar
        def _(act):
            def bias_qk(b):
                for n in range(2 * DT):
                    after(act, qk_proj, b, 2 * DT, n + 1)
                    nc.scalar.activation(QKf[:, n, :], PS[:, bank_qk(n), :], ACT.Identity,
                                         bias=BQK[:, n:n + 1]).then_inc(qk_biased, 1)

            def body(b, first, last):
                for s in range(STEPS):
                    for pair in range(2):
                        after(act, scoredT, b, 2 * STEPS, 2 * s + pair + 1)
                        if s >= RING:
                            after(act, pv_done, b, STEPS, s - RING + 1)
                        nc.scalar.activation(PT[:, s % RING, 2 * pair:2 * pair + 2, :],
                                             PS[:, 2 * pair:2 * pair + 2, :], ACT.Exp,
                                             scale=SCALE).then_inc(exp_done, 1)
                if not last:
                    bias_qk(b + 1)
                for c in range(DT):
                    after(act, x2_turned, b, DT, c + 1)
                    nc.scalar.activation(X2hi[:, c, :], PS[:, 4 + c, :], ACT.Identity).then_inc(x2_hi_done, 1)
                for m in range(HT):
                    after(act, ffn1, b, 2 * HT, 2 * m + 1)
                    if m >= 2:
                        after(act, up_done, b, HT, m - 1)
                    nc.scalar.activation(SIL[:, m % 2, :], PS[:, bank1(m, 0), :], ACT.Silu,
                                         scale=SC[:, 0, m:m + 1]).then_inc(gate_done, 1)
                for layer, full in ((2, hidC_full), (3, hidA_full)):
                    for m in range(HT):
                        after(act, ffn23, b, 2 * HT, (layer - 2) * HT + m + 1)
                        nc.scalar.activation(full[:, m, :], PS[:, bank23(m), :], ACT.Gelu,
                                             scale=SC[:, layer, m:m + 1]).then_inc(gelu_done, 1)

            for n, (w, src) in enumerate(((W1f, w1T), (W2f, w2T), (G1f, h1T), (G2f, h2T), (W3f, w3T))):
                act.dma_start(w[:], src.rearrange("(t p) m -> p t m", p=P)).then_inc(w_in[n], 16)
            act.wait_ge(consts_in, 16 * N_CONSTS)
            bias_qk(0)
            per_batch(act, body)

        @block.vector
        def _(dve):
            nc.vector.memset(ST_f[SPLIT:ROWS, :, :, 1, :], 1.0).then_inc(consts_set, 1)
            nc.vector.memset(VXT[:], 1.0).then_inc(consts_set, 1)
            nc.vector.memset(ONESF[:], 1.0).then_inc(consts_set, 1)
            nc.vector.memset(NEGM[:], 0.0).then_inc(consts_set, 1)

            def split_qk(b):
                for n in range(2 * DT):
                    after(dve, qk_biased, b, 2 * DT, n + 1)
                    nc.vector.tensor_copy(QKhi[:, n, :], QKf[:, n, :]).then_inc(qk_hi_done, 1)
                    after(dve, qk_hi_done, b, 2 * DT, n + 1)
                    nc.vector.tensor_tensor(QKlo[:, n, :], QKf[:, n, :], QKhi_f[:, n, :],
                                            ALU.subtract).then_inc(qk_split, 1)

            def take_v(b):
                after(dve, v_proj, b, QT, QT)
                nc.vector.tensor_tensor(Vt[:], PS[:, 4:8, 0:D],
                                        BV[:].rearrange("p (a d) -> p a d", a=1).to_broadcast([P, QT, D]),
                                        ALU.add).then_inc(v_taken, 1)
                after(dve, v_taken, b, 1, 1)
                nc.vector.tensor_scalar(Vm[:], Vt[:], 0.0, None, ALU.min).then_inc(v_step, 1)
                after(dve, v_step, b, 1, 1)
                for t in range(QT):
                    nc.vector.scalar_tensor_tensor(
                        out=VXT[:, t, 0:H * VW].rearrange("p (h e) -> p h e", e=VW)[:, :, 0:HD],
                        in0=Vt[:, t, :].rearrange("p (h e) -> p h e", e=HD), scalar=0.0,
                        in1=Vm[:, t, :].rearrange("p (h e) -> p h e", e=HD),
                        op0=ALU.max, op1=ALU.add).then_inc(v_ready, 1)

            def row_max(b, h):
                for pair in range(2):
                    after(dve, scored, b, 2 * H, 2 * h + pair + 1)
                    nc.vector.tensor_reduce(NEGM[:, h * QT + 2 * pair:h * QT + 2 * pair + 2],
                                            PS[:, 2 * pair:2 * pair + 2, :], AX.X, ALU.max,
                                            negate=True).then_inc(maxed, 1)

            def split_max(b):
                after(dve, max_turned, b, 1, 1)
                after(dve, max_stored, b, 16, 0)
                nc.vector.tensor_copy(MROW[:, 0, :], PS[0:H * QT, 0, 0:P]).then_inc(max_hi_done, 1)
                after(dve, max_hi_done, b, 1, 1)
                nc.vector.tensor_tensor(MROW[:, 1, :], PS[0:H * QT, 0, 0:P], MROW_f[:, 0, :],
                                        ALU.subtract).then_inc(max_split, 1)

            def guard(b, s):
                for pair in range(2):
                    after(dve, exp_done, b, 2 * STEPS, 2 * s + pair + 1)
                    p = PT[:, s % RING, 2 * pair:2 * pair + 2, :]
                    nc.vector.tensor_scalar(p, p, 0.0, None, ALU.max).then_inc(probs_ready, 1)

            def take_z(b, g):
                after(dve, pv_done, b, STEPS, QT * (g + 1))
                nc.vector.transpose(ZB[:], PS[:, 4 + g % 2, :].rearrange("p (r c) -> p c r", c=HD)).then_inc(zT_taken, 1)
                after(dve, zT_taken, b, NQUAD, g + 1)
                nc.vector.reciprocal(REC[:].rearrange("p (c e) -> p c e", e=1), ZB[:, :, HD:HD + 1]).then_inc(rec_done, 1)
                after(dve, rec_done, b, NQUAD, g + 1)
                nc.vector.tensor_tensor(
                    Z[:, g, :].rearrange("p (c e) -> p c e", e=HD), ZB[:, :, 0:HD],
                    REC[:].rearrange("p (c e) -> p c e", e=1).to_broadcast([P, HD, HD]), ALU.mult).then_inc(z_taken, 1)

            def rstd(tiles, step, b, n, count):
                done = [count]
                y, nv, t = NY[:, tiles], NV[:, tiles], NT[:, tiles]

                def then(ins, wait=True):
                    done[0] += 1
                    ins.then_inc(step, 1)
                    if wait:
                        after(dve, step, b, n, done[0])

                then(nc.vector.tensor_scalar(y, MV[:, tiles, 1], EPS, None, ALU.add))
                then(nc.vector.tensor_scalar(NI[:, tiles], NY_i[:, tiles], 1, None, ALU.logical_shift_right), False)
                then(nc.vector.tensor_scalar(nv, y, -0.5, None, ALU.mult))
                then(nc.vector.tensor_scalar(NY_i[:, tiles], NI[:, tiles], -1.0, RSQRT_SEED, ALU.mult, ALU.add))
                for _ in range(NEWTON):
                    then(nc.vector.tensor_tensor(t, y, y, ALU.mult))
                    then(nc.vector.tensor_tensor(t, t, nv, ALU.mult))
                    then(nc.vector.scalar_tensor_tensor(out=y, in0=t, scalar=1.5, in1=y,
                                                        op0=ALU.add, op1=ALU.mult))
                return done[0]

            def normalize(src, dst, t):
                return nc.vector.tensor_scalar(dst[:, t, :], src[:, t, :], MV[:, t, 0:1], NY[:, t:t + 1],
                                               ALU.subtract, ALU.mult)

            RS = 4 + 3 * NEWTON
            N_NORM = 2 + RS
            N_TILE = 2 * N_NORM + 7
            N12 = QT * N_TILE

            def norm_steps(b, count):
                n = [count]

                def then(ins, wait=True):
                    n[0] += 1
                    ins.then_inc(norm_step, 1)
                    if wait:
                        after(dve, norm_step, b, N12, n[0])

                return n, then

            def statistics(src, t, b, n, then):
                then(nc.vector.bn_stats(STAT[:, t, :], src[:, t, :]))
                nc.vector.memset(NT[:, t:t + 1], 0.0)
                then(nc.vector.bn_aggr(MV[:, t, :], STAT[:, t, :]))
                n[0] = rstd(slice(t, t + 1), norm_step, b, N12, n[0])

            def first_norm(b, t):
                n, then = norm_steps(b, t * N_TILE)
                after(dve, z_taken, b, NQUAD, t + 1)
                then(nc.vector.tensor_scalar(T1[:, t, :], Z[:, t, :], 0.0, None, ALU.min))
                then(nc.vector.scalar_tensor_tensor(out=Z[:, t, :], in0=Z[:, t, :], scalar=0.0, in1=T1[:, t, :],
                                                    op0=ALU.max, op1=ALU.add))
                after(dve, x_in, b, 16, 16)
                then(nc.vector.tensor_tensor(Z[:, t, :], Z[:, t, :], X[:, t, :], ALU.add))
                statistics(Z, t, b, n, then)
                then(normalize(Z, Z, t))
                then(nc.vector.tensor_tensor(Z[:, t, :], Z[:, t, :], GAM[:], ALU.mult))
                then(nc.vector.tensor_tensor(Z[:, t, :], Z[:, t, :], BET[:], ALU.add))
                then(nc.vector.tensor_tensor(X[:, t, :], Z[:, t, :], X[:, t, :], ALU.add), False)
                assert n[0] == t * N_TILE + N_TILE - N_NORM

            def second_norm(b, t):
                n, then = norm_steps(b, t * N_TILE + N_TILE - N_NORM)
                after(dve, norm_step, b, N12, n[0])
                statistics(X, t, b, n, then)
                assert n[0] == (t + 1) * N_TILE
                normalize(X, X, t).then_inc(x2_ready, 1)

            def split_x2(b):
                for c in range(DT):
                    after(dve, x2_hi_done, b, DT, c + 1)
                    nc.vector.tensor_tensor(X2lo[:, c, :], PS[:, 4 + c, :], X2hif[:, c, :],
                                            ALU.subtract).then_inc(x2_split, 1)

            def last_norm(b):
                n3 = QT + QT + QT + RS
                after(dve, x2_ready, b, QT, QT)
                for t in range(QT):
                    after(dve, y_done, b, QT, t + 1)
                    nc.vector.tensor_tensor(T1[:, t, :], PS[:, bank23(t), 0:D], S3[:], ALU.mult).then_inc(y_taken, 1)
                    after(dve, y_taken, b, QT, t + 1)
                    nc.vector.tensor_tensor(X[:, t, :], X[:, t, :], T1[:, t, :], ALU.add).then_inc(last_step, 1)
                    after(dve, last_step, b, n3, 2 * t + 1)
                    nc.vector.bn_stats(STAT[:, t, :], X[:, t, :]).then_inc(last_step, 1)
                after(dve, last_step, b, n3, 2 * QT)
                nc.vector.memset(NT[:, 0:1], 0.0)
                for t in range(QT):
                    nc.vector.bn_aggr(MV[:, t, :], STAT[:, t, :]).then_inc(last_step, 1)
                after(dve, last_step, b, n3, 3 * QT)
                rstd(slice(0, QT), last_step, b, n3, 3 * QT)
                after(dve, out_stored, b, 16, 0)
                for t in range(QT):
                    normalize(X, OUT, t).then_inc(out_ready, 1)

            def body(b, first, last):
                for s in range(STEPS):
                    guard(b, s)
                    if first and s >= STEPS - len(PIECES):
                        look_at_weights(s - (STEPS - len(PIECES)))
                    g, ago = divmod(s - (QT - 1 + LAG), QT)
                    if ago == 1 and g >= 0:
                        take_z(b, g)
                    if ago == 2 and g >= 0:
                        first_norm(b, g)
                    if ago == 3 and g >= 0:
                        second_norm(b, g)
                for g in range(NQUAD):
                    last_ago = STEPS - 1 - (QT - 1 + LAG) - QT * g
                    if last_ago < 1:
                        take_z(b, g)
                    if last_ago < 2:
                        first_norm(b, g)
                    if last_ago < 3:
                        second_norm(b, g)
                if first:
                    sum_up_bits()
                if not last:
                    split_qk(b + 1)
                    take_v(b + 1)
                if first:
                    dve.wait_ge(bits_summed, 1)
                    nc.vector.tensor_scalar(FLAG[:], PS[0:1, 0, 0:1], 0.5, None, ALU.is_ge).then_inc(flag_set, 1)
                split_x2(b)
                for m in range(HT):
                    after(dve, gate_done, b, HT, m + 1)
                    after(dve, ffn1, b, 2 * HT, 2 * m + 2)
                    if m == 0 and not last:
                        after(dve, rows_stored, b, 8 * 16, 16 * 16)
                    nc.vector.scalar_tensor_tensor(out=hidA_full[:, m, :], in0=PS[:, bank1(m, 1), :],
                                                   scalar=SC[:, 1, m:m + 1], in1=SIL[:, m % 2, :],
                                                   op0=ALU.mult, op1=ALU.mult).then_inc(up_done, 1)
                    after(dve, up_done, b, HT, m + 1)
                    nc.vector.tensor_copy(hidA_hi[:, m, :], hidA_full[:, m, :]).then_inc(hi_done, 1)
                for layer, full, hi in ((2, hidC_full, hidC_hi), (3, hidA_full, hidA_hi)):
                    for m in range(HT):
                        if not last:
                            for h in heads_beside(layer, m):
                                row_max(b + 1, h)
                            if (layer, m) == (3, TURN_MAX_AT):
                                split_max(b + 1)
                        after(dve, gelu_done, b, 2 * HT, (layer - 2) * HT + m + 1)
                        nc.vector.tensor_copy(hi[:, m, :], full[:, m, :]).then_inc(hi_done, 1)
                last_norm(b)

            def look_at_weights(n):
                which, at = PIECES[n]
                w = (W1f, W2f, G1f, G2f, W3f)[which]
                w = w[:].bitcast(I32).rearrange("p a b -> p (a b)")
                dve.wait_ge(w_in[which], 16)
                if n:
                    dve.wait_ge(bits_seen, n)
                nc.vector.tensor_scalar(LOW[:], w[:, at:at + PIECE], 0xFFF, None,
                                        ALU.bitwise_and).then_inc(bits_cut, 1)
                dve.wait_ge(bits_cut, n + 1)
                nc.vector.tensor_reduce(BITS[:, n:n + 1], LOW[:], AX.X, ALU.max).then_inc(bits_seen, 1)

            def sum_up_bits():
                dve.wait_ge(bits_seen, len(PIECES))
                nc.vector.tensor_reduce(BITS1[:], BITS[:, 0:len(PIECES)], AX.X, ALU.max).then_inc(bits_f, 1)
                dve.wait_ge(bits_f, 1)
                nc.vector.tensor_copy(BITF[:], BITS1[:]).then_inc(bits_f, 1)

            dve.wait_ge(consts_in, 16 * N_CONSTS)
            split_qk(0)
            take_v(0)
            for h in range(H):
                row_max(0, h)
            split_max(0)
            per_batch(dve, body)

        @block.tensor
        def _(pe):
            def project(b):
                after(pe, xT_in, b, 16, 16)
                for n in range(2 * DT):
                    if n < DT:
                        after(pe, y_taken, b, QT, -QT)
                    else:
                        after(pe, zT_taken, b, NQUAD, n % 2 - 1)
                    w, c = (WQ, WK)[n // DT], n % DT
                    for k in range(DT):
                        ins = nc.tensor.matmul(PS[:, bank_qk(n), :], w[:, k, c * P:(c + 1) * P], XT[:, k, :],
                                               start=(k == 0), stop=(k == DT - 1))
                    ins.then_inc(qk_proj, 1)
                for n, t in enumerate((2, 3, 0, 1)):
                    after(pe, qk_biased, b, 2 * DT, n + 1)
                    for k in range(DT):
                        ins = nc.tensor.matmul(PS[:, 4 + t, 0:D], XT[:, k, t * P:(t + 1) * P], WV[:, k, :],
                                               start=(k == 0), stop=(k == DT - 1))
                    ins.then_inc(v_proj, 1)

            def row_scores(b, h):
                if h % QUAD == 0:
                    after_stack(pe, b, h // QUAD, False)
                for pair in range(2):
                    if h:
                        after(pe, maxed, b, 2 * H, 2 * h + pair - 1)
                    else:
                        after(pe, exp_done, b, 2 * H, 0)
                    for qt in (2 * pair, 2 * pair + 1):
                        ins = nc.tensor.matmul(PS[:, qt, :],
                                               ST[0:SPLIT, (h // QUAD) % 2, h % QUAD, 0, qt * P:(qt + 1) * P],
                                               ST[0:SPLIT, (h // QUAD) % 2, h % QUAD, 1, :],
                                               start=True, stop=True)
                    ins.then_inc(scored, 1)

            def turn_max(b):
                after(pe, maxed, b, 2 * H, 2 * H)
                nc.tensor.transpose(PS[:, 0, 0:P], NEGM[:], ID[:]).then_inc(max_turned, 1)

            def scores_T(b, s):
                g, kt = divmod(s, QT)
                if kt == 0:
                    after_stack(pe, b, g, True)
                for pair in range(2):
                    if s:
                        after(pe, exp_done, b, 2 * STEPS, 2 * s + pair - 1)
                    else:
                        after(pe, max_split, b, 1, 1)
                        after(pe, maxed, b, 2 * H, 2 * H)
                    for j in (2 * pair, 2 * pair + 1):
                        ins = nc.tensor.matmul(PS[:, j, :], ST[:, g % 2, j, 1, kt * P:(kt + 1) * P],
                                               ST[:, g % 2, j, 0, :], start=True, stop=True)
                    ins.then_inc(scoredT, 1)

            def values(b, s):
                g, kt = divmod(s, QT)
                bank = 4 + g % 2
                if kt == 0:
                    if g < 2:
                        after(pe, y_taken, b, QT, 0)
                        after(pe, v_taken, b, 1, 1)
                    else:
                        after(pe, zT_taken, b, NQUAD, g - 1)
                after(pe, probs_ready, b, 2 * STEPS, 2 * s + 2)
                after(pe, v_ready, b, QT, QT)
                lo, hi = kt * P, (kt + 1) * P
                for j in range(QUAD):
                    nc.tensor.matmul(PS[32 * j:32 * j + 32, bank, lo:S], ONE[:, 0:32],
                                     PT[:, s % RING, j, lo:S], start=(kt == 0), stop=False,
                                     skip_group_check=True)
                if kt:
                    for j in range(QUAD):
                        h = g * QUAD + j
                        nc.tensor.matmul(PS[32 * j:32 * j + 32, bank, 0:lo], VXT[:, kt, VW * h:VW * h + 32],
                                         PT[:, s % RING, j, 0:lo], start=False, stop=False,
                                         skip_group_check=True)
                after(pe, diag_ready, b, STEPS, s + 1)
                for j in range(QUAD):
                    h = g * QUAD + j
                    ins = nc.tensor.matmul(PS[32 * j:32 * j + HD, bank, lo:hi], VXT[:, kt, VW * h:VW * h + HD],
                                           PM[:, s % 2, j, :], start=False, stop=(kt == QT - 1),
                                           skip_group_check=True)
                ins.then_inc(pv_done, 1)

            def turn_x2(b, last):
                if last:
                    after(pe, zT_taken, b, NQUAD, NQUAD)
                else:
                    after(pe, v_taken, b, 1, 2)
                for t in range(QT):
                    after(pe, x2_ready, b, QT, t + 1)
                    for c in range(DT):
                        ins = nc.tensor.transpose(PS[:, 4 + c, t * P:(t + 1) * P], X[:, t, c * P:(c + 1) * P], ID[:])
                        if t == QT - 1:
                            ins.then_inc(x2_turned, 1)

            def feed_forward(b, last, general):
                chunk = [0]

                def product(out, kts, weights, data, when, signal, done, per_chunk, swapped=False):
                    for k in range(kts):
                        if when is not None:
                            after(pe, lo_done, b, 3 * HT, when + k + 1)
                        if general and k % per_chunk == 0:
                            c = chunk[0]
                            chunk[0] += 1
                            after(pe, chunk_in[c % 2], b, CHUNKS // 2 * 16, 16 * (c // 2 + 1))
                        for part in (0, 1):
                            d = data(k)[2 * general + part]
                            if general:
                                width = D if swapped else P
                                w = WB[:, c % 2, (k % per_chunk) * width:(k % per_chunk + 1) * width]
                            else:
                                w = weights(k)
                            ins = nc.tensor.matmul(out, d if swapped else w, w if swapped else d,
                                                   start=(k == 0 and part == 0), stop=(k == kts - 1 and part == 1))
                        if general and k % per_chunk == per_chunk - 1 and k < kts - 1:
                            ins.then_inc(chunk_used, 1)
                    ins.then_inc(signal, done)
                    if general:
                        nc.tensor.drain().then_inc(chunk_used, 1)

                for m in range(HT):
                    for which, w in ((0, W1), (1, W2)):
                        if m == 0:
                            after(pe, y_taken if last else v_taken, b, QT if last else 1, 0 if last else 2)
                            after(pe, x2_split, b, DT, DT)
                        if m >= 2:
                            after(pe, (gate_done, up_done)[which], b, HT, m - 1)
                        product(PS[:, bank1(m, which), :], DT, lambda k: w[:, k, m * P:(m + 1) * P],
                                lambda k: (X2hi[:, k, :], X2lo[:, k, :], X2hif[:, k, :], X2lof[:, k, :]),
                                None, ffn1, 1, DT)
                for layer, w, (hi, lo, hif, lof) in (
                        (2, G1, (hidA_hi, hidA_lo, hidA_hif, hidA_lof)),
                        (3, G2, (hidC_hi, hidC_lo, hidC_hif, hidC_lof))):
                    for m in range(HT):
                        if not last:
                            for h in heads_beside(layer, m):
                                row_scores(b + 1, h)
                            if (layer, m) == (3, TURN_MAX_AT):
                                turn_max(b + 1)
                        if layer == 2 and m < 4:
                            after(pe, (gate_done, up_done)[m % 2], b, HT, 7 + m // 2)
                        else:
                            after(pe, gelu_done, b, 2 * HT, (layer - 2) * HT + m - 3)
                        product(PS[:, bank23(m), :], HT, lambda k: w[:, k, m * P:(m + 1) * P],
                                lambda k: (hi[:, k, :], lo[:, k, :], hif[:, k, :], lof[:, k, :]),
                                (layer - 2) * HT if m == 0 else None, ffn23, 1, 4)
                for t in range(QT):
                    tok = slice(t * P, (t + 1) * P)
                    after(pe, gelu_done, b, 2 * HT, HT + 5 + t)
                    product(PS[:, bank23(t), 0:D], HT, lambda k: W3[:, k, :],
                            lambda k: (hidA_hi[:, k, tok], hidA_lo[:, k, tok], hidA_hif[:, k, tok], hidA_lof[:, k, tok]),
                            2 * HT if t == 0 else None, y_done, 1, 2, swapped=True)

            pe.wait_ge(consts_in, 16 * N_CONSTS)
            pe.wait_ge(qkv_w_in, 16 * 3)
            pe.wait_ge(consts_set, 4)
            project(0)
            for h in range(H):
                row_scores(0, h)
            turn_max(0)
            pe.wait_ge(masks_set, 4)
            inexact = []

            def body(b, first, last):
                for s in range(STEPS):
                    scores_T(b, s)
                    if s >= LAG:
                        values(b, s - LAG)
                for s in range(STEPS - LAG, STEPS):
                    values(b, s)
                if not last:
                    project(b + 1)
                if first:
                    pe.wait_ge(bits_f, 2)
                    nc.tensor.matmul(PS[0:1, 0, 0:1], BITF[:], ONESF[:], start=True, stop=True).then_inc(bits_summed, 1)
                    pe.wait_ge(flag_set, 1)
                    inexact.append(pe.value_load(FLAG[0:1, 0:1], min_val=0, max_val=1))
                    pe.wait_ge(w_rounded, 5)
                turn_x2(b, last)
                with pe.If(inexact[0]):
                    feed_forward(b, last, True)
                with pe.Else():
                    feed_forward(b, last, False)

            per_batch(pe, body)


_INS = {
    "x": (B * S, D), "xT": (B * D, S), "wqT": (D, D), "wkT": (D, D), "wvT": (D, D), "bqk": (P, 2 * DT),
    "bv": (D,), "gamma": (D,), "beta": (D,), "w1T": (D, DH), "w2T": (D, DH), "h1T": (DH, DH), "h2T": (DH, DH),
    "scales": (P, 4 * HT), "w3T": (DH, D), "s3": (D,), "ident": (P, P),
}


def kernel(L0_attn_embedded, L0_attn_Wq, L0_attn_bq, L0_attn_Wk, L0_attn_bk, L0_attn_Wv, L0_attn_bv,
           L0_attn_gamma, L0_attn_beta, L0_ffn_w1_w, L0_ffn_w1_s, L0_ffn_w2_w, L0_ffn_w2_s, L0_ffn_h1_w,
           L0_ffn_h1_s, L0_ffn_h2_w, L0_ffn_h2_s, L0_ffn_w3_w, L0_ffn_w3_s):
    import numpy as np
    import concourse.bacc as bacc
    from concourse.bass_utils import run_bass_kernel_spmd

    x = np.asarray(L0_attn_embedded)

    def turned(w):
        return np.ascontiguousarray(np.asarray(w).T)

    def dim_major(w):
        w = np.asarray(w)
        return w.reshape(H, HD, *w.shape[1:]).swapaxes(0, 1).reshape(w.shape)

    def by_partition(*vectors):
        return np.ascontiguousarray(np.concatenate([np.asarray(v).reshape(-1, P) for v in vectors]).T)

    arrays = {
        "x": np.ascontiguousarray(x.reshape(B * S, D)),
        "xT": np.ascontiguousarray(x.transpose(0, 2, 1).reshape(B * D, S)),
        "wqT": turned(dim_major(L0_attn_Wq)), "wkT": turned(dim_major(L0_attn_Wk)), "wvT": turned(L0_attn_Wv),
        "bqk": by_partition(dim_major(L0_attn_bq), dim_major(L0_attn_bk)), "bv": np.asarray(L0_attn_bv),
        "gamma": np.asarray(L0_attn_gamma), "beta": np.asarray(L0_attn_beta),
        "w1T": turned(L0_ffn_w1_w), "w2T": turned(L0_ffn_w2_w),
        "h1T": turned(L0_ffn_h1_w), "h2T": turned(L0_ffn_h2_w), "w3T": turned(L0_ffn_w3_w),
        "scales": by_partition(L0_ffn_w1_s, L0_ffn_w2_s, L0_ffn_h1_s, L0_ffn_h2_s),
        "s3": np.asarray(L0_ffn_w3_s),
        "ident": np.eye(P, dtype=np.float32),
    }
    nc = bacc.Bacc("TRN2", target_bir_lowering=False, num_devices=1,
                   dynamic_dma_scratch_size=1024)
    args = {name: nc.dram_tensor(name + "_dram", shape, F32, kind="ExternalInput").ap()
            for name, shape in _INS.items()}
    args["out"] = nc.dram_tensor("out_dram", (B * S, D), F32, kind="ExternalOutput").ap()
    build_program(nc, **args)
    ran = run_bass_kernel_spmd(nc, [{name + "_dram": arrays[name] for name in _INS}], core_ids=[0])
    return ran.results[0]["out_dram"].reshape(B, S, D)
```

```python
from contextlib import ExitStack

import concourse.bass as bass
from concourse import mybir

F32 = mybir.dt.float32
F32R = mybir.dt.float32r
I32 = mybir.dt.int32
ALU = mybir.AluOpType
ACT = mybir.ActivationFunctionType
AX = mybir.AxisListType

P = 128
B, S, D = 8, 512, 256
H, HD = 16, 16
DH = 1024
QT = S // P
DT = D // P
HT = DH // P
QUAD = 4
NQUAD = H // QUAD
SPLIT = 4 * HD
ROWS = SPLIT + 2
VW = HD + 1
VX = 288
EPS = 1e-5
PIECE = 1024
STAGES = 3
SCALE = 1.0 / float(S) ** 0.5
RSQRT_SEED = float(0x5F3759DF)
TINY = 1e-30
NEWTON = 3
STEPS = NQUAD * QT
RING = 4
LAG = 2
PAIRS = 2 * H
PAIRS1 = 2
X2_CUT = 3 * P
KB = 1024


def build_program(nc, x, xT, wqT, wkT, wvT, bqk, bv, gamma, beta, w1T, w2T, h1T, h2T, scales,
                  w3T, s3, ident, out):
    base = (nc.sbuf_base + 63) // 64 * 64
    top = [base]

    def place(name, shape, dt, at=None):
        size = 4
        for n in shape[1:]:
            size *= n
        where = top[0] if at is None else at
        if at is None:
            top[0] += (size + 31) // 32 * 32
        return nc.alloc_sbuf_tensor_at(name, shape, dt, offset=where)

    def both(name, shape, at=None):
        rounded = place(name, shape, F32R, at)
        return rounded, rounded[:].bitcast(F32)

    W1 = place("w1", [P, DT, DH], F32R)
    W2 = place("w2", [P, DT, DH], F32R)
    G1 = place("g1", [P, HT, DH], F32R)
    G2 = place("g2", [P, HT, DH], F32R)
    W3 = place("w3", [P, HT, D], F32R)
    WQ = place("wq", [P, DT, D], F32)
    WK = place("wk", [P, DT, D], F32)
    WV = place("wv", [P, DT, D], F32)

    A = top[0]
    hidA_hi, hidA_hif = both("hidA_hi", [P, HT, S])
    hidA_full = place("hidA_full", [P, HT, S], F32, top[0])
    hidA_lo, hidA_lof = both("hidA_lo", [P, HT, S])
    PT = place("probsT", [P, RING, QUAD, S], F32, A)
    QKf = place("qk_full", [P, 2 * DT, S], F32, A)
    QKhi, QKhi_f = both("qk_hi", [P, 2 * DT, S], A + 8 * KB)
    QKlo, QKlo_f = both("qk_lo", [P, 2 * DT, S], A + 16 * KB)
    C = top[0]
    hidC_hi, hidC_hif = both("hidC_hi", [P, HT, S])
    hidC_full = place("hidC_full", [P, HT, S], F32, top[0])
    hidC_lo, hidC_lof = both("hidC_lo", [P, HT, S])
    X2hi, X2hif = both("x2T_hi", [P, DT, S], C)
    X2lo, X2lof = both("x2T_lo", [P, DT, S], C + 4 * KB)
    SIL = place("gate", [P, 2, S], F32, C + 8 * KB)
    XT = place("xT_sb", [P, DT, S], F32, C + 12 * KB)
    PM = place("diag_probs", [P, 2, QUAD, P], F32, C + 16 * KB)
    ZB = place("z_blocks", [P, HD, 2 * HD], F32, C + 20 * KB)
    RAW = [place(f"raw_weights{n}", [P, PIECE], F32, C + 4 * KB * n) for n in range(STAGES)]
    Z = place("z", [P, QT, D], F32, C + 24 * KB)
    XB = place("x_plus_beta", [P, QT, D], F32, C + 28 * KB)
    T1 = place("scaled_y", [P, QT, D], F32, C + 28 * KB)

    ST, ST_f = both("stacks", [ROWS, 2, QUAD, 2, S])
    VXT = place("v_ones", [P, QT, VX], F32)
    X = place("x_tok", [P, QT, D], F32)
    Vm = place("v_negative", [P, QT, D], F32, top[0])
    OUT = place("out_tok", [P, QT, D], F32)
    GAM = place("gamma_b", [P, D], F32)
    BET = place("beta_b", [P, D], F32)
    BV = place("bv_b", [P, D], F32)
    S3 = place("s3_b", [P, D], F32)
    ID = place("ident_sb", [P, P], F32)
    MASK = place("mask", [P, P], F32)
    ONE = place("ones_col", [P, 32], F32)
    WB = place("w_chunk", [P, 2, S], F32)
    BQK = place("bqk", [P, 2 * DT], F32)
    SC = place("scales", [P, 4, HT], F32)
    NEGM = place("neg_max", [P, P], F32)
    MROW, MROW_f = both("max_rows", [H * QT, 2, P])
    REC = place("rec", [P, HD], F32)
    STAT = place("stats", [P, QT, 6], F32)
    MV = place("mean_var", [P, QT, 2], F32)
    NV = place("neg_half_var", [P, QT], F32)
    NY = place("rstd", [P, QT], F32)
    NY_i = NY[:].bitcast(I32)
    NT = place("newton_tmp", [P, QT], F32)
    CHANGED = place("changed", [P, 32], F32)
    CHANGED1 = place("changed_row", [P, 1], F32)
    ONESF = place("ones_f", [P, 1], F32)
    FLAG = place("inexact", [1, 1], I32)
    assert top[0] <= nc.sbuf_usable_end, top[0] - nc.sbuf_usable_end

    qk_rows = nc.dram_tensor("qk_rows", [4, D, 2, S], F32, kind="Internal").ap()
    max_rows = nc.dram_tensor("max_rows_d", [2, H * QT * P], F32, kind="Internal").ap()

    with ExitStack() as ctx:
        PS = ctx.enter_context(nc.psum_tensor("PS", [P, 8, 512], F32))

        def sem(name):
            return ctx.enter_context(nc.semaphore(name))

        consts_in, qk_w_in, v_w_in, bqk_in = sem("consts_in"), sem("qk_w_in"), sem("v_w_in"), sem("bqk_in")
        piece_in = [sem(f"piece_in{n}") for n in range(STAGES)]
        xT_in, x_in = sem("xT_in"), sem("x_in")
        rows_stored, max_stored, out_stored = sem("rows_stored"), sem("max_stored"), sem("out_stored")
        stack_in = [sem("stack_in0"), sem("stack_in1")]
        chunk_in = [sem("chunk_in0"), sem("chunk_in1")]
        consts_set, w_rounded, compared = sem("consts_set"), sem("w_rounded"), sem("compared")
        row_counted, counted, flag_set = sem("row_counted"), sem("counted"), sem("flag_set")
        masks_set = sem("masks_set")
        scored = sem("scored")
        maxed = sem("maxed")
        max_turned, max_hi_done, max_split = sem("max_turned"), sem("max_hi_done"), sem("max_split")
        scoredT = sem("scoredT")
        exp_done = sem("exp_done")
        probs_ready = sem("probs_ready")
        diag_ready = sem("diag_ready")
        pv_done = sem("pv_done")
        zT_taken = sem("zT_taken")
        rec_done, z_taken = sem("rec_done"), sem("z_taken")
        qk_proj, qk_full_done, qk_biased, qk_split = sem("qk_proj"), sem("qk_full_done"), sem("qk_biased"), sem("qk_split")
        v_proj, v_taken, v_step, v_ready = sem("v_proj"), sem("v_taken"), sem("v_step"), sem("v_ready")
        norm_step, last_step, beta_added = sem("norm_step"), sem("last_step"), sem("beta_added")
        x2_ready, x2_turned, x2_hi_done, x2_split = sem("x2_ready"), sem("x2_turned"), sem("x2_hi_done"), sem("x2_split")
        ffn1, gate_done, up_done = sem("ffn1"), sem("gate_done"), sem("up_done")
        ffn23, gelu_done = sem("ffn23"), sem("gelu_done")
        hi_done, lo_done = sem("hi_done"), sem("lo_done")
        y_done, y_taken, out_ready = sem("y_done"), sem("y_taken"), sem("out_ready")
        chunk_used = sem("chunk_used")
        block = ctx.enter_context(nc.Block())

        def per_batch(engine, body):
            body(0, True, False)
            with engine.Fori(1, B - 1) as b:
                body(b, False, False)
            body(B - 1, False, True)

        def after(engine, s, b, n, count):
            value = n * b + count
            if isinstance(value, int) and value <= 0:
                return
            engine.wait_ge(s, value)

        LOADS_S, LOADS_T = 16, 32
        IN_PER_BATCH = 2 * LOADS_S + 2 * LOADS_T

        def after_stack(engine, b, group, transposed):
            had = (2 * LOADS_S + (group // 2) * LOADS_T + LOADS_T) if transposed else (group // 2 + 1) * LOADS_S
            after(engine, stack_in[group % 2], b, IN_PER_BATCH, had)

        def pair_beside(layer, m, half):
            if layer == 1:
                return (m - 4) // 2 if half == 0 and m in (4, 6) else None
            n = PAIRS1 + ((layer - 2) * HT + m) * 2 + half
            return n if n < PAIRS else None

        TURN_MAX_AT = (3, HT - 1, 1)

        def bank1(m, which):
            return 4 + (2 * m + 2 + which) % 4

        def bank23(m):
            return 4 + (m + 2) % 4

        def bank_qk(n):
            return (6, 7, 0, 1)[n]

        CHUNKS = 2 * HT + 2 * 2 * HT + QT * 4

        def x2_part(part):
            if part == 0:
                return PS[:, 4:4 + DT, 0:X2_CUT], slice(0, X2_CUT)
            return PS[:, 6, 0:DT * P].rearrange("p (c s) -> p c s", c=DT), slice(X2_CUT, S)

        PIECES = [(src, w, k, PIECE // w.shape[2])
                  for src, w in ((w1T, W1), (w2T, W2), (h1T, G1), (h2T, G2), (w3T, W3))
                  for k in range(0, w.shape[1], PIECE // w.shape[2])]
        EARLY = 8
        N_CONSTS = 6

        def pieces_at(s):
            return range(EARLY + 2 * s, min(EARLY + 2 * s + 2, len(PIECES)))

        COUNT_AT = (len(PIECES) - EARLY + 1) // 2 + 1

        @block.sync
        def _(sp):
            sp.dma_start(XT[:], xT[0:D, :].rearrange("(t p) s -> p t s", p=P)).then_inc(xT_in, 16)
            sp.dma_start(WK[:], wkT.rearrange("(t p) m -> p t m", p=P)).then_inc(qk_w_in, 16)
            sp.dma_start(WV[:], wvT.rearrange("(t p) m -> p t m", p=P)).then_inc(v_w_in, 16)
            sp.dma_start(SC[:], scales.rearrange("p (n t) -> p n t", n=4)).then_inc(consts_in, 16)
            sp.dma_start(BV[:], bv.rearrange("(a d) -> a d", a=1).to_broadcast([P, D])).then_inc(consts_in, 16)
            sp.dma_start(ID[:], ident).then_inc(consts_in, 16)
            for t, src in ((GAM, gamma), (BET, beta), (S3, s3)):
                sp.dma_start(t[:], src.rearrange("(a d) -> a d", a=1).to_broadcast([P, D])).then_inc(consts_in, 16)

            def load_stacks(b, group, transposed):
                n, back = 2 * H, 2 * QUAD * (group - 1)
                if group >= 2:
                    after(sp, scoredT if transposed else scored, b, n, back)
                else:
                    after(sp, scored if transposed else scoredT, b, n, back + n - (0 if transposed else n))
                if group == 0 and not transposed:
                    after(sp, rows_stored, b, 8 * 16, 8 * 16)
                rows = qk_rows.rearrange("r (d h) a s -> (r d) h a s", d=HD)
                sp.dma_start(ST_f[0:SPLIT, group % 2, :, :, :],
                             rows[:, group * QUAD:(group + 1) * QUAD, :, :]).then_inc(stack_in[group % 2], 16)
                if transposed:
                    if group == 0:
                        after(sp, max_stored, b, 16, 16)
                    sp.dma_start(ST_f[SPLIT:ROWS, group % 2, :, 0, :],
                                 max_rows[:, group * QUAD * S:(group + 1) * QUAD * S].rearrange(
                                     "r (h s) -> r h s", h=QUAD)).then_inc(stack_in[group % 2], 16)

            def store_rows(b):
                after(sp, qk_split, b, 2 * DT, 2 * DT)
                for a, parts in enumerate(((QKhi_f, QKhi_f, QKlo_f, QKlo_f), (QKhi_f, QKlo_f, QKhi_f, QKlo_f))):
                    for r, part in enumerate(parts):
                        sp.dma_start(qk_rows[r, :, a, :].rearrange("(t p) s -> p t s", p=P),
                                     part[:, a * DT:(a + 1) * DT, :]).then_inc(rows_stored, 16)

            def chunks(b, first, count, source):
                for c in range(first, first + count):
                    after(sp, chunk_used, b, CHUNKS, c - 1)
                    src, shape = source(c - first)
                    sp.dma_start(WB[:, c % 2, 0:shape[0] * shape[1]].rearrange("p (k m) -> p k m", m=shape[1]),
                                 src).then_inc(chunk_in[c % 2], 16)

            def feed_forward(b, last, general):
                def hidden(src, m):
                    return lambda c: (src.rearrange("(k p) m -> p k m", p=P)[:, 4 * c:4 * c + 4, m * P:(m + 1) * P], (4, P))

                def head_group(g):
                    if not last:
                        load_stacks(b + 1, g, False)

                if not general:
                    if not last:
                        for g in range(NQUAD):
                            load_stacks(b + 1, g, False)
                    return
                head_group(0)
                head_group(1)
                c0 = 0
                for m in range(HT):
                    for w in (w1T, w2T):
                        chunks(b, c0, 1, lambda c: (w.rearrange("(k p) m -> p k m", p=P)[:, :, m * P:(m + 1) * P], (DT, P)))
                        c0 += 1
                for layer, w in ((2, h1T), (3, h2T)):
                    for m in range(HT):
                        if (layer, m) == (2, 4):
                            head_group(2)
                        if (layer, m) == (3, 0):
                            head_group(3)
                        chunks(b, c0, 2, hidden(w, m))
                        c0 += 2
                for t in range(QT):
                    chunks(b, c0, 4, lambda c: (w3T.rearrange("(k p) m -> p k m", p=P)[:, 2 * c:2 * c + 2, :], (2, D)))
                    c0 += 4

            store_rows(0)
            for g in range(NQUAD):
                load_stacks(0, g, False)
            after(sp, max_split, 0, 1, 1)
            sp.dma_start(max_rows.rearrange("r (q p) -> q r p", p=P), MROW_f).then_inc(max_stored, 16)
            inexact = []

            def body(b, first, last):
                here = b * S if isinstance(b, int) else sp.snap(b * S)
                before = (b - 1) * S if isinstance(b, int) else sp.snap((b - 1) * S)
                next_dims = (b + 1) * D if isinstance(b, int) else sp.snap((b + 1) * D)
                if not last:
                    if first:
                        sp.wait_ge(v_proj, QT)
                    else:
                        after(sp, y_done, b, QT, -QT + 1)
                    sp.dma_start(XT[:], xT[bass.ds(next_dims, D), :].rearrange("(t p) s -> p t s", p=P)).then_inc(xT_in, 16)
                for g in range(2):
                    load_stacks(b, g, True)
                after(sp, out_ready, b, QT, 0)
                if not first:
                    sp.dma_start(out[bass.ds(before, S), :].rearrange("(t p) d -> p t d", p=P), OUT[:]).then_inc(out_stored, 16)
                sp.dma_start(X[:], x[bass.ds(here, S), :].rearrange("(t p) d -> p t d", p=P)).then_inc(x_in, 16)
                for g in range(2, NQUAD):
                    load_stacks(b, g, True)
                if not last:
                    store_rows(b + 1)
                if first:
                    sp.wait_ge(flag_set, 1)
                    inexact.append(sp.value_load(FLAG[0:1, 0:1], min_val=0, max_val=1))
                with sp.If(inexact[0]):
                    feed_forward(b, last, True)
                if not last:
                    with sp.Else():
                        feed_forward(b, last, False)
                if not last:
                    after(sp, max_split, b, 1, 2)
                    sp.dma_start(max_rows.rearrange("r (q p) -> q r p", p=P), MROW_f).then_inc(max_stored, 16)

            per_batch(sp, body)
            sp.wait_ge(out_ready, QT * B)
            sp.dma_start(out[(B - 1) * S:B * S, :].rearrange("(t p) d -> p t d", p=P), OUT[:]).then_inc(out_stored, 16)
            sp.wait_ge(out_stored, 16 * B)
            sp.wait_ge(rows_stored, 8 * 16 * B)
            sp.wait_ge(max_stored, 16 * B)

        @block.gpsimd
        def _(pool):
            nc.gpsimd.memset(MASK[:], 1.0).then_inc(masks_set, 1)
            nc.gpsimd.memset(ONE[:], 0.0).then_inc(masks_set, 1)
            pool.wait_ge(masks_set, 2)
            nc.gpsimd.affine_select(out=MASK[:], in_=MASK[:], compare_op=ALU.is_ge, fill=0.0, base=0,
                                    pattern=[[-1, P]], channel_multiplier=1).then_inc(masks_set, 1)
            nc.gpsimd.memset(ONE[:, HD:HD + 1], 1.0).then_inc(masks_set, 1)

            def low_part(n_before, b, full, hi, lo, m):
                after(pool, hi_done, b, 3 * HT, n_before + m + 1)
                nc.gpsimd.tensor_tensor(lo[:, m, :], full[:, m, :], hi[:, m, :], ALU.subtract).then_inc(lo_done, 1)

            def masks(b, s):
                kt = s % QT
                after(pool, probs_ready, b, 2 * STEPS, 2 * s + 2)
                after(pool, pv_done, b, STEPS, s - 1)
                nc.gpsimd.tensor_tensor(PM[:, s % 2, :, :], PT[:, s % RING, :, kt * P:(kt + 1) * P],
                                        MASK[:].rearrange("p (a m) -> p a m", a=1).to_broadcast([P, QUAD, P]),
                                        ALU.mult).then_inc(diag_ready, 1)

            def split_qk(b):
                for n in range(2 * DT):
                    after(pool, qk_biased, b, 2 * DT, n + 1)
                    nc.gpsimd.tensor_tensor(QKlo[:, n, :], QKf[:, n, :], QKhi_f[:, n, :],
                                            ALU.subtract).then_inc(qk_split, 1)

            def body(b, first, last):
                for s in range(STEPS):
                    masks(b, s)
                    if s == 1:
                        after(pool, x_in, b, 16, 16)
                        nc.gpsimd.tensor_tensor(XB[:], X[:], BET[:].rearrange("p (a d) -> p a d", a=1).to_broadcast(
                            [P, QT, D]), ALU.add).then_inc(beta_added, 1)
                if not last:
                    split_qk(b + 1)
                for m in range(HT):
                    low_part(0, b, hidA_full, hidA_hif, hidA_lo, m)
                for m in range(HT):
                    low_part(HT, b, hidC_full, hidC_hif, hidC_lo, m)
                for m in range(HT):
                    low_part(2 * HT, b, hidA_full, hidA_hif, hidA_lo, m)

            split_qk(0)
            pool.wait_ge(consts_in, 16 * N_CONSTS)
            per_batch(pool, body)

        @block.scalar
        def _(act):
            def bias_qk(b):
                for n in range(2 * DT):
                    after(act, qk_proj, b, 2 * DT, n + 1)
                    nc.scalar.activation(QKf[:, n, :], PS[:, bank_qk(n), :], ACT.Identity,
                                         bias=BQK[:, n:n + 1]).then_inc(qk_full_done, 1)
                    nc.scalar.activation(QKhi[:, n, :], PS[:, bank_qk(n), :], ACT.Identity,
                                         bias=BQK[:, n:n + 1]).then_inc(qk_biased, 1)

            def load_piece(n):
                src, w, k, kts = PIECES[n]
                act.dma_start(RAW[n % STAGES][:].rearrange("p (k m) -> p k m", k=kts),
                              src.rearrange("(k p) m -> p k m", p=P)[:, k:k + kts, :]).then_inc(piece_in[n % STAGES], 16)

            def round_piece(n):
                if n + 2 < len(PIECES):
                    if n:
                        act.wait_ge(compared, n)
                    load_piece(n + 2)
                _, w, k, kts = PIECES[n]
                act.wait_ge(piece_in[n % STAGES], 16 * (n // STAGES + 1))
                nc.scalar.activation(w[:, k:k + kts, :], RAW[n % STAGES][:].rearrange("p (k m) -> p k m", k=kts),
                                     ACT.Identity).then_inc(w_rounded, 1)

            def body(b, first, last):
                for s in range(STEPS):
                    for pair in range(2):
                        after(act, scoredT, b, 2 * STEPS, 2 * s + pair + 1)
                        if s >= RING:
                            after(act, pv_done, b, STEPS, s - RING + 1)
                        nc.scalar.activation(PT[:, s % RING, 2 * pair:2 * pair + 2, :],
                                             PS[:, 2 * pair:2 * pair + 2, :], ACT.Exp,
                                             scale=SCALE).then_inc(exp_done, 1)
                    if first:
                        for n in pieces_at(s):
                            round_piece(n)
                if not last:
                    bias_qk(b + 1)
                for part in range(2):
                    after(act, x2_turned, b, 2, part + 1)
                    src, dst = x2_part(part)
                    nc.scalar.activation(X2hi[:, :, dst], src, ACT.Identity).then_inc(x2_hi_done, 1)
                for m in range(HT):
                    after(act, ffn1, b, 2 * HT, 2 * m + 1)
                    if m >= 2:
                        after(act, up_done, b, HT, m - 1)
                    nc.scalar.activation(SIL[:, m % 2, :], PS[:, bank1(m, 0), :], ACT.Silu,
                                         scale=SC[:, 0, m:m + 1]).then_inc(gate_done, 1)
                for layer, full in ((2, hidC_full), (3, hidA_full)):
                    for m in range(HT):
                        after(act, ffn23, b, 2 * HT, (layer - 2) * HT + m + 1)
                        nc.scalar.activation(full[:, m, :], PS[:, bank23(m), :], ACT.Gelu,
                                             scale=SC[:, layer, m:m + 1]).then_inc(gelu_done, 1)

            act.dma_start(WQ[:], wqT.rearrange("(t p) m -> p t m", p=P)).then_inc(qk_w_in, 16)
            act.dma_start(BQK[:], bqk).then_inc(bqk_in, 16)
            load_piece(0)
            load_piece(1)
            act.wait_ge(bqk_in, 16)
            bias_qk(0)
            act.wait_ge(consts_in, 16 * N_CONSTS)
            for n in range(EARLY):
                round_piece(n)
            per_batch(act, body)

        @block.vector
        def _(dve):
            nc.vector.memset(ST_f[SPLIT:ROWS, :, :, 1, :], 1.0).then_inc(consts_set, 1)
            nc.vector.memset(VXT[:], 1.0).then_inc(consts_set, 1)
            nc.vector.memset(ONESF[:], 1.0).then_inc(consts_set, 1)
            nc.vector.memset(NEGM[:], 0.0).then_inc(consts_set, 1)

            def take_v(b):
                after(dve, v_proj, b, QT, QT)
                after(dve, pv_done, b, STEPS, 0)
                nc.vector.tensor_tensor(
                    v_part(slice(0, QT)),
                    PS[:, 2:4, :].rearrange("p a (t h e) -> p (a t) h e", t=2, e=HD),
                    BV[:].rearrange("p (a h e) -> p a h e", a=1, e=HD).to_broadcast([P, QT, H, HD]),
                    ALU.add).then_inc(v_taken, 1)

            def v_part(t):
                return VXT[:, t, 0:H * VW].rearrange("p t (h e) -> p t h e", e=VW)[:, :, :, 0:HD]

            def guard_v(b, t):
                after(dve, v_taken, b, 1, 1)
                if t == 0:
                    after(dve, out_stored, b, 16, -16)
                v, negative = v_part(slice(t, t + 1)), Vm[:, t:t + 1, :].rearrange("p t (h e) -> p t h e", e=HD)
                nc.vector.tensor_scalar(negative, v, 0.0, None, ALU.min).then_inc(v_step, 1)
                after(dve, v_step, b, QT, t + 1)
                nc.vector.scalar_tensor_tensor(out=v, in0=v, scalar=0.0, in1=negative,
                                               op0=ALU.max, op1=ALU.add).then_inc(v_ready, 1)

            def row_max(b, pair):
                h, half = divmod(pair, 2)
                after(dve, scored, b, PAIRS, pair + 1)
                nc.vector.tensor_reduce(NEGM[:, h * QT + 2 * half:h * QT + 2 * half + 2],
                                        PS[:, 2 * half:2 * half + 2, :], AX.X, ALU.max,
                                        negate=True).then_inc(maxed, 1)

            def split_max(b):
                after(dve, max_turned, b, 1, 1)
                after(dve, max_stored, b, 16, 0)
                nc.vector.tensor_copy(MROW[:, 0, :], PS[0:H * QT, 0, 0:P]).then_inc(max_hi_done, 1)
                after(dve, max_hi_done, b, 1, 1)
                nc.vector.tensor_tensor(MROW[:, 1, :], PS[0:H * QT, 0, 0:P], MROW_f[:, 0, :],
                                        ALU.subtract).then_inc(max_split, 1)

            def guard(b, s):
                for pair in range(2):
                    after(dve, exp_done, b, 2 * STEPS, 2 * s + pair + 1)
                    p = PT[:, s % RING, 2 * pair:2 * pair + 2, :]
                    nc.vector.tensor_scalar(p, p, 0.0, None, ALU.max).then_inc(probs_ready, 1)

            def take_z(b, g):
                after(dve, pv_done, b, STEPS, QT * (g + 1))
                nc.vector.transpose(ZB[:], PS[:, 4 + g % 2, :].rearrange("p (r c) -> p c r", c=HD)).then_inc(zT_taken, 1)
                after(dve, zT_taken, b, NQUAD, g + 1)
                nc.vector.tensor_scalar(REC[:].rearrange("p (c e) -> p c e", e=1), ZB[:, :, HD:HD + 1], TINY, None,
                                        ALU.max).then_inc(rec_done, 1)
                after(dve, rec_done, b, 2 * NQUAD, 2 * g + 1)
                nc.vector.reciprocal(REC[:], REC[:]).then_inc(rec_done, 1)
                after(dve, rec_done, b, 2 * NQUAD, 2 * g + 2)
                nc.vector.tensor_tensor(
                    Z[:, g, :].rearrange("p (c e) -> p c e", e=HD), ZB[:, :, 0:HD],
                    REC[:].rearrange("p (c e) -> p c e", e=1).to_broadcast([P, HD, HD]), ALU.mult).then_inc(z_taken, 1)

            def rstd(tiles, step, b, n, count, meanwhile=None):
                done = [count]
                y, nv, t = NY[:, tiles], NV[:, tiles], NT[:, tiles]
                one = tiles.stop - tiles.start == 1

                def then(ins, wait=True):
                    done[0] += 1
                    ins.then_inc(step, 1)
                    if wait:
                        after(dve, step, b, n, done[0])

                then(nc.vector.tensor_scalar(y, MV[:, tiles, 1], EPS, None, ALU.add))
                then(nc.vector.tensor_scalar(nv, y, -0.5, None, ALU.mult), False)
                then(nc.vector.tensor_scalar(NY_i[:, tiles], NY_i[:, tiles], -0.5, RSQRT_SEED, ALU.mult, ALU.add), False)
                if meanwhile is not None:
                    then(meanwhile(), False)
                after(dve, step, b, n, done[0])
                for _ in range(NEWTON):
                    if one:
                        then(nc.vector.scalar_tensor_tensor(out=t, in0=y, scalar=nv, in1=y,
                                                            op0=ALU.mult, op1=ALU.mult))
                    else:
                        then(nc.vector.tensor_tensor(t, y, y, ALU.mult))
                        then(nc.vector.tensor_tensor(t, t, nv, ALU.mult))
                    then(nc.vector.scalar_tensor_tensor(out=y, in0=t, scalar=1.5, in1=y,
                                                        op0=ALU.add, op1=ALU.mult))
                return done[0]

            def normalize(src, dst, t):
                return nc.vector.tensor_scalar(dst[:, t, :], src[:, t, :], MV[:, t, 0:1], NY[:, t:t + 1],
                                               ALU.subtract, ALU.mult)

            RS1, RS = 3 + 2 * NEWTON, 3 + 3 * NEWTON
            N_NORM = 2 + RS1
            N_TILE = 2 * N_NORM + 3
            N12 = QT * N_TILE

            def norm_steps(b, count):
                n = [count]

                def then(ins, wait=True):
                    n[0] += 1
                    ins.then_inc(norm_step, 1)
                    if wait:
                        after(dve, norm_step, b, N12, n[0])

                return n, then

            def statistics(src, t, b, n, then, meanwhile=None):
                then(nc.vector.bn_stats(STAT[:, t, :], src[:, t, :]))
                nc.vector.memset(NT[:, t:t + 1], 0.0)
                then(nc.vector.bn_aggr(MV[:, t, :], STAT[:, t, :]))
                n[0] = rstd(slice(t, t + 1), norm_step, b, N12, n[0], meanwhile)

            def first_norm(b, t):
                n, then = norm_steps(b, t * N_TILE)
                after(dve, z_taken, b, NQUAD, t + 1)
                if t == 0:
                    after(dve, x_in, b, 16, 16)
                then(nc.vector.tensor_tensor(Z[:, t, :], Z[:, t, :], X[:, t, :], ALU.add))
                statistics(Z, t, b, n, then, lambda: nc.vector.scalar_tensor_tensor(
                    out=Z[:, t, :], in0=Z[:, t, :], scalar=MV[:, t, 0:1], in1=GAM[:], op0=ALU.subtract, op1=ALU.mult))
                if t == 0:
                    after(dve, beta_added, b, 1, 1)
                then(nc.vector.scalar_tensor_tensor(out=X[:, t, :], in0=Z[:, t, :], scalar=NY[:, t:t + 1],
                                                    in1=XB[:, t, :], op0=ALU.mult, op1=ALU.add), False)
                assert n[0] == t * N_TILE + N_TILE - N_NORM

            def second_norm(b, t):
                n, then = norm_steps(b, t * N_TILE + N_TILE - N_NORM)
                after(dve, norm_step, b, N12, n[0])
                statistics(X, t, b, n, then)
                assert n[0] == (t + 1) * N_TILE
                normalize(X, X, t).then_inc(x2_ready, 1)

            def split_x2(b):
                for part in range(2):
                    after(dve, x2_hi_done, b, 2, part + 1)
                    src, dst = x2_part(part)
                    nc.vector.tensor_tensor(X2lo[:, :, dst], src, X2hif[:, :, dst], ALU.subtract).then_inc(x2_split, 1)

            def last_norm(b):
                n3 = QT + QT + QT + RS
                after(dve, x2_ready, b, QT, QT)
                for t in range(QT):
                    after(dve, y_done, b, QT, t + 1)
                    nc.vector.tensor_tensor(T1[:, t, :], PS[:, bank23(t), 0:D], S3[:], ALU.mult).then_inc(y_taken, 1)
                    after(dve, y_taken, b, QT, t + 1)
                    nc.vector.tensor_tensor(X[:, t, :], X[:, t, :], T1[:, t, :], ALU.add).then_inc(last_step, 1)
                    after(dve, last_step, b, n3, 2 * t + 1)
                    nc.vector.bn_stats(STAT[:, t, :], X[:, t, :]).then_inc(last_step, 1)
                after(dve, last_step, b, n3, 2 * QT)
                nc.vector.memset(NT[:, 0:1], 0.0)
                for t in range(QT):
                    nc.vector.bn_aggr(MV[:, t, :], STAT[:, t, :]).then_inc(last_step, 1)
                after(dve, last_step, b, n3, 3 * QT)
                rstd(slice(0, QT), last_step, b, n3, 3 * QT)
                after(dve, out_stored, b, 16, 0)
                for t in range(QT):
                    normalize(X, OUT, t).then_inc(out_ready, 1)

            def body(b, first, last):
                for s in range(STEPS):
                    guard(b, s)
                    if first:
                        for n in pieces_at(s):
                            compare(n)
                        if s == COUNT_AT - 1:
                            count_changes()
                    g, ago = divmod(s - (QT - 1 + LAG), QT)
                    if ago == 1 and g >= 0:
                        take_z(b, g)
                    if ago == 2 and g >= 0:
                        first_norm(b, g)
                    if ago == 3 and g >= 0:
                        second_norm(b, g)
                for g in range(NQUAD):
                    last_ago = STEPS - 1 - (QT - 1 + LAG) - QT * g
                    if last_ago < 1:
                        take_z(b, g)
                    if last_ago < 2:
                        first_norm(b, g)
                    if last_ago < 3:
                        second_norm(b, g)
                split_x2(b)
                if not last:
                    take_v(b + 1)
                for m in range(HT):
                    if not last and pair_beside(1, m, 0) is not None:
                        row_max(b + 1, pair_beside(1, m, 0))
                    after(dve, gate_done, b, HT, m + 1)
                    after(dve, ffn1, b, 2 * HT, 2 * m + 2)
                    if m == 0 and not last:
                        after(dve, rows_stored, b, 8 * 16, 16 * 16)
                    nc.vector.scalar_tensor_tensor(out=hidA_full[:, m, :], in0=PS[:, bank1(m, 1), :],
                                                   scalar=SC[:, 1, m:m + 1], in1=SIL[:, m % 2, :],
                                                   op0=ALU.mult, op1=ALU.mult).then_inc(up_done, 1)
                    after(dve, up_done, b, HT, m + 1)
                    nc.vector.tensor_copy(hidA_hi[:, m, :], hidA_full[:, m, :]).then_inc(hi_done, 1)
                for layer, full, hi in ((2, hidC_full, hidC_hi), (3, hidA_full, hidA_hi)):
                    for m in range(HT):
                        if not last:
                            for half in range(2):
                                if pair_beside(layer, m, half) is not None:
                                    row_max(b + 1, pair_beside(layer, m, half))
                                if (layer, m, half) == TURN_MAX_AT:
                                    split_max(b + 1)
                        after(dve, gelu_done, b, 2 * HT, (layer - 2) * HT + m + 1)
                        nc.vector.tensor_copy(hi[:, m, :], full[:, m, :]).then_inc(hi_done, 1)
                        if not last and layer == 2 and m < QT:
                            guard_v(b + 1, m)
                last_norm(b)

            def compare(n):
                _, w, k, kts = PIECES[n]
                raw = RAW[n % STAGES][:].rearrange("p (k m) -> p k m", k=kts)
                dve.wait_ge(w_rounded, n + 1)
                nc.vector.scalar_tensor_tensor(out=raw, in0=raw, scalar=1.0, in1=w[:, k:k + kts, :].bitcast(F32),
                                               op0=ALU.mult, op1=ALU.not_equal,
                                               accum_out=CHANGED[:, n:n + 1]).then_inc(compared, 1)

            def count_changes():
                dve.wait_ge(compared, len(PIECES))
                nc.vector.tensor_reduce(CHANGED1[:], CHANGED[:, 0:len(PIECES)], AX.X, ALU.add).then_inc(row_counted, 1)
                dve.wait_ge(counted, 1)
                nc.vector.tensor_scalar(FLAG[:], PS[0:1, 7, 0:1], 0.5, None, ALU.is_ge).then_inc(flag_set, 1)

            dve.wait_ge(consts_in, 16 * N_CONSTS)
            dve.wait_ge(consts_set, 4)
            take_v(0)
            for t in range(QT):
                guard_v(0, t)
            for n in range(EARLY):
                compare(n)
            for pair in range(PAIRS):
                row_max(0, pair)
            split_max(0)
            per_batch(dve, body)

        @block.tensor
        def _(pe):
            def project(b):
                after(pe, xT_in, b, 16, 16)
                for n in range(2 * DT):
                    if n == 0:
                        after(pe, y_taken, b, QT, -QT)
                    if n == DT:
                        after(pe, exp_done, b, 2 * STEPS, 0)
                    w, c = (WQ, WK)[n // DT], n % DT
                    for k in range(DT):
                        ins = nc.tensor.matmul(PS[:, bank_qk(n), :], w[:, k, c * P:(c + 1) * P], XT[:, k, :],
                                               start=(k == 0), stop=(k == DT - 1))
                    ins.then_inc(qk_proj, 1)
                if isinstance(b, int) and b == 0:
                    pe.wait_ge(v_w_in, 16)
                for t in range(QT):
                    for k in range(DT):
                        ins = nc.tensor.matmul(PS[:, 2 + t // 2, t % 2 * D:(t % 2 + 1) * D],
                                               XT[:, k, t * P:(t + 1) * P], WV[:, k, :],
                                               start=(k == 0), stop=(k == DT - 1))
                    ins.then_inc(v_proj, 1)

            def row_scores(b, pair):
                h, half = divmod(pair, 2)
                if h % QUAD == 0 and half == 0:
                    after_stack(pe, b, h // QUAD, False)
                if pair == 0:
                    after(pe, qk_biased, b, 2 * DT, 2 * DT)
                elif pair == 1:
                    after(pe, v_taken, b, 1, 1)
                else:
                    after(pe, maxed, b, PAIRS, pair - 1)
                for qt in (2 * half, 2 * half + 1):
                    ins = nc.tensor.matmul(PS[:, qt, :],
                                           ST[0:SPLIT, (h // QUAD) % 2, h % QUAD, 0, qt * P:(qt + 1) * P],
                                           ST[0:SPLIT, (h // QUAD) % 2, h % QUAD, 1, :],
                                           start=True, stop=True)
                ins.then_inc(scored, 1)

            def turn_max(b):
                after(pe, maxed, b, 2 * H, 2 * H)
                nc.tensor.transpose(PS[:, 0, 0:P], NEGM[:], ID[:]).then_inc(max_turned, 1)

            def scores_T(b, s):
                g, kt = divmod(s, QT)
                if kt == 0:
                    after_stack(pe, b, g, True)
                for pair in range(2):
                    if s:
                        after(pe, exp_done, b, 2 * STEPS, 2 * s + pair - 1)
                    else:
                        after(pe, max_split, b, 1, 1)
                        after(pe, maxed, b, 2 * H, 2 * H)
                    for j in (2 * pair, 2 * pair + 1):
                        ins = nc.tensor.matmul(PS[:, j, :], ST[:, g % 2, j, 1, kt * P:(kt + 1) * P],
                                               ST[:, g % 2, j, 0, :], start=True, stop=True)
                    ins.then_inc(scoredT, 1)

            def values(b, s):
                g, kt = divmod(s, QT)
                bank = 4 + g % 2
                if kt == 0:
                    if g < 2:
                        after(pe, y_taken, b, QT, 0)
                    else:
                        after(pe, zT_taken, b, NQUAD, g - 1)
                after(pe, probs_ready, b, 2 * STEPS, 2 * s + 2)
                after(pe, v_ready, b, QT, QT)
                lo, hi = kt * P, (kt + 1) * P
                for j in range(QUAD):
                    nc.tensor.matmul(PS[32 * j:32 * j + 32, bank, lo:S], ONE[:, 0:32],
                                     PT[:, s % RING, j, lo:S], start=(kt == 0), stop=False,
                                     skip_group_check=True)
                if kt:
                    for j in range(QUAD):
                        h = g * QUAD + j
                        nc.tensor.matmul(PS[32 * j:32 * j + 32, bank, 0:lo], VXT[:, kt, VW * h:VW * h + 32],
                                         PT[:, s % RING, j, 0:lo], start=False, stop=False,
                                         skip_group_check=True)
                after(pe, diag_ready, b, STEPS, s + 1)
                for j in range(QUAD):
                    h = g * QUAD + j
                    ins = nc.tensor.matmul(PS[32 * j:32 * j + HD, bank, lo:hi], VXT[:, kt, VW * h:VW * h + HD],
                                           PM[:, s % 2, j, :], start=False, stop=(kt == QT - 1),
                                           skip_group_check=True)
                ins.then_inc(pv_done, 1)

            def turn_x2(b, last):
                after(pe, zT_taken, b, NQUAD, NQUAD)
                for t in range(QT):
                    part = t // (X2_CUT // P)
                    if part and not last:
                        after(pe, qk_biased, b, 2 * DT, 2 * DT + 1)
                    after(pe, x2_ready, b, QT, t + 1)
                    for c in range(DT):
                        dst = x2_part(part)[0][:, c, (t * P) % X2_CUT:(t * P) % X2_CUT + P]
                        ins = nc.tensor.transpose(dst, X[:, t, c * P:(c + 1) * P], ID[:])
                    if (t + 1) * P in (X2_CUT, S):
                        ins.then_inc(x2_turned, 1)

            def feed_forward(b, last, general):
                chunk = [0]

                def beside(layer, m, half):
                    if last:
                        return
                    if pair_beside(layer, m, half) is not None:
                        row_scores(b + 1, pair_beside(layer, m, half))
                    if (layer, m, half) == TURN_MAX_AT:
                        turn_max(b + 1)

                def product(out, kts, weights, data, when, signal, done, per_chunk, swapped=False, halfway=None):
                    for k in range(kts):
                        if halfway is not None and k == kts // 2:
                            halfway()
                        if when is not None:
                            after(pe, lo_done, b, 3 * HT, when + k + 1)
                        if general and k % per_chunk == 0:
                            c = chunk[0]
                            chunk[0] += 1
                            after(pe, chunk_in[c % 2], b, CHUNKS // 2 * 16, 16 * (c // 2 + 1))
                        for part in (0, 1):
                            d = data(k)[2 * general + part]
                            if general:
                                width = D if swapped else P
                                w = WB[:, c % 2, (k % per_chunk) * width:(k % per_chunk + 1) * width]
                            else:
                                w = weights(k)
                            ins = nc.tensor.matmul(out, d if swapped else w, w if swapped else d,
                                                   start=(k == 0 and part == 0), stop=(k == kts - 1 and part == 1))
                        if general and k % per_chunk == per_chunk - 1 and k < kts - 1:
                            ins.then_inc(chunk_used, 1)
                    ins.then_inc(signal, done)
                    if general:
                        nc.tensor.drain().then_inc(chunk_used, 1)

                for m in range(HT):
                    beside(1, m, 0)
                    for which, w in ((0, W1), (1, W2)):
                        if m == 0:
                            after(pe, x2_split, b, 2, 2)
                            if not last:
                                after(pe, qk_biased, b, 2 * DT, 2 * DT + 2)
                        if m >= 2:
                            after(pe, (gate_done, up_done)[which], b, HT, m - 1)
                        product(PS[:, bank1(m, which), :], DT, lambda k: w[:, k, m * P:(m + 1) * P],
                                lambda k: (X2hi[:, k, :], X2lo[:, k, :], X2hif[:, k, :], X2lof[:, k, :]),
                                None, ffn1, 1, DT)
                for layer, w, (hi, lo, hif, lof) in (
                        (2, G1, (hidA_hi, hidA_lo, hidA_hif, hidA_lof)),
                        (3, G2, (hidC_hi, hidC_lo, hidC_hif, hidC_lof))):
                    for m in range(HT):
                        beside(layer, m, 0)
                        if layer == 2 and m < 4:
                            after(pe, (gate_done, up_done)[m % 2], b, HT, 7 + m // 2)
                        else:
                            after(pe, gelu_done, b, 2 * HT, (layer - 2) * HT + m - 3)
                        product(PS[:, bank23(m), :], HT, lambda k: w[:, k, m * P:(m + 1) * P],
                                lambda k: (hi[:, k, :], lo[:, k, :], hif[:, k, :], lof[:, k, :]),
                                (layer - 2) * HT if m == 0 else None, ffn23, 1, 4,
                                halfway=lambda: beside(layer, m, 1))
                for t in range(QT):
                    tok = slice(t * P, (t + 1) * P)
                    after(pe, gelu_done, b, 2 * HT, HT + 5 + t)
                    product(PS[:, bank23(t), 0:D], HT, lambda k: W3[:, k, :],
                            lambda k: (hidA_hi[:, k, tok], hidA_lo[:, k, tok], hidA_hif[:, k, tok], hidA_lof[:, k, tok]),
                            2 * HT if t == 0 else None, y_done, 1, 2, swapped=True)

            pe.wait_ge(qk_w_in, 16 * 2)
            project(0)
            pe.wait_ge(consts_set, 4)
            for pair in range(PAIRS):
                row_scores(0, pair)
            pe.wait_ge(consts_in, 16 * N_CONSTS)
            turn_max(0)
            pe.wait_ge(masks_set, 4)
            inexact = []

            def body(b, first, last):
                for s in range(STEPS):
                    if first and s == COUNT_AT:
                        pe.wait_ge(row_counted, 1)
                        nc.tensor.matmul(PS[0:1, 7, 0:1], CHANGED1[:], ONESF[:], start=True, stop=True).then_inc(counted, 1)
                    scores_T(b, s)
                    if s >= LAG:
                        values(b, s - LAG)
                for s in range(STEPS - LAG, STEPS):
                    values(b, s)
                if first:
                    pe.wait_ge(flag_set, 1)
                    inexact.append(pe.value_load(FLAG[0:1, 0:1], min_val=0, max_val=1))
                    pe.wait_ge(w_rounded, len(PIECES))
                if not last:
                    project(b + 1)
                turn_x2(b, last)
                with pe.If(inexact[0]):
                    feed_forward(b, last, True)
                with pe.Else():
                    feed_forward(b, last, False)

            per_batch(pe, body)


_INS = {
    "x": (B * S, D), "xT": (B * D, S), "wqT": (D, D), "wkT": (D, D), "wvT": (D, D), "bqk": (P, 2 * DT),
    "bv": (D,), "gamma": (D,), "beta": (D,), "w1T": (D, DH), "w2T": (D, DH), "h1T": (DH, DH), "h2T": (DH, DH),
    "scales": (P, 4 * HT), "w3T": (DH, D), "s3": (D,), "ident": (P, P),
}


def kernel(L0_attn_embedded, L0_attn_Wq, L0_attn_bq, L0_attn_Wk, L0_attn_bk, L0_attn_Wv, L0_attn_bv,
           L0_attn_gamma, L0_attn_beta, L0_ffn_w1_w, L0_ffn_w1_s, L0_ffn_w2_w, L0_ffn_w2_s, L0_ffn_h1_w,
           L0_ffn_h1_s, L0_ffn_h2_w, L0_ffn_h2_s, L0_ffn_w3_w, L0_ffn_w3_s):
    import numpy as np
    import concourse.bacc as bacc
    from concourse.bass_utils import run_bass_kernel_spmd

    x = np.asarray(L0_attn_embedded)

    def turned(w):
        return np.ascontiguousarray(np.asarray(w).T)

    def dim_major(w):
        w = np.asarray(w)
        return w.reshape(H, HD, *w.shape[1:]).swapaxes(0, 1).reshape(w.shape)

    def by_partition(*vectors):
        return np.ascontiguousarray(np.concatenate([np.asarray(v).reshape(-1, P) for v in vectors]).T)

    arrays = {
        "x": np.ascontiguousarray(x.reshape(B * S, D)),
        "xT": np.ascontiguousarray(x.transpose(0, 2, 1).reshape(B * D, S)),
        "wqT": turned(dim_major(L0_attn_Wq)), "wkT": turned(dim_major(L0_attn_Wk)), "wvT": turned(L0_attn_Wv),
        "bqk": by_partition(dim_major(L0_attn_bq), dim_major(L0_attn_bk)), "bv": np.asarray(L0_attn_bv),
        "gamma": np.asarray(L0_attn_gamma), "beta": np.asarray(L0_attn_beta),
        "w1T": turned(L0_ffn_w1_w), "w2T": turned(L0_ffn_w2_w),
        "h1T": turned(L0_ffn_h1_w), "h2T": turned(L0_ffn_h2_w), "w3T": turned(L0_ffn_w3_w),
        "scales": by_partition(L0_ffn_w1_s, L0_ffn_w2_s, L0_ffn_h1_s, L0_ffn_h2_s),
        "s3": np.asarray(L0_ffn_w3_s),
        "ident": np.eye(P, dtype=np.float32),
    }
    nc = bacc.Bacc("TRN2", target_bir_lowering=False, num_devices=1,
                   dynamic_dma_scratch_size=1024)
    args = {name: nc.dram_tensor(name + "_dram", shape, F32, kind="ExternalInput").ap()
            for name, shape in _INS.items()}
    args["out"] = nc.dram_tensor("out_dram", (B * S, D), F32, kind="ExternalOutput").ap()
    build_program(nc, **args)
    ran = run_bass_kernel_spmd(nc, [{name + "_dram": arrays[name] for name in _INS}], core_ids=[0])
    return ran.results[0]["out_dram"].reshape(B, S, D)
```

```python
from contextlib import ExitStack

import concourse.bass as bass
from concourse import mybir

F32 = mybir.dt.float32
F32R = mybir.dt.float32r
I32 = mybir.dt.int32
ALU = mybir.AluOpType
ACT = mybir.ActivationFunctionType
AX = mybir.AxisListType

P = 128
B, S, D = 8, 512, 256
H, HD = 16, 16
DH = 1024
QT = S // P
DT = D // P
HT = DH // P
QUAD = 4
NQUAD = H // QUAD
SPLIT = 4 * HD
ROWS = SPLIT + 2
VW = HD + 1
VX = 288
EPS = 1e-5
PIECE = 1024
BEHIND = 2
STAGES = 6
SCALE = 1.0 / float(S) ** 0.5
RSQRT_SEED = float(0x5F3759DF)
TINY = 1e-30
NEWTON = 3
STEPS = NQUAD * QT
RING = 4
LAG = 2
X_AT = 5
MAXES = H * QT // 2
SAFE_SQUARES = 1e34
PAIRS = 2 * H
X2_CUT = 3 * P
KB = 1024


def build_program(nc, x, xT, wqT, wkT, wvT, bqk, bv, gamma, beta, w1T, w2T, h1T, h2T, scales,
                  w3T, s3, ident, out):
    base = (nc.sbuf_base + 63) // 64 * 64
    top = [base]

    def place(name, shape, dt, at=None):
        size = 4
        for n in shape[1:]:
            size *= n
        where = top[0] if at is None else at
        if at is None:
            top[0] += (size + 31) // 32 * 32
        return nc.alloc_sbuf_tensor_at(name, shape, dt, offset=where)

    def both(name, shape, at=None):
        rounded = place(name, shape, F32R, at)
        return rounded, rounded[:].bitcast(F32)

    W1 = place("w1", [P, DT, DH], F32R)
    W2 = place("w2", [P, DT, DH], F32R)
    G1 = place("g1", [P, HT, DH], F32R)
    G2 = place("g2", [P, HT, DH], F32R)
    W3 = place("w3", [P, HT, D], F32R)
    WQ = place("wq", [P, DT, D], F32)
    WK = place("wk", [P, DT, D], F32)
    WV = place("wv", [P, DT, D], F32)

    A = top[0]
    hidA_hi, hidA_hif = both("hidA_hi", [P, HT, S])
    hidA_full = place("hidA_full", [P, HT, S], F32, top[0])
    hidA_lo, hidA_lof = both("hidA_lo", [P, HT, S])
    Z = place("z", [P, QT, D], F32, A)
    XB = place("x_plus_beta", [P, QT, D], F32, A + 4 * KB)
    PM = place("diag_probs", [P, 2, QUAD, P], F32, A + 24 * KB)
    QKlo, QKlo_f = both("qk_lo", [P, 2 * DT, S], A + 8 * KB)
    QKf = place("qk_full", [P, 2 * DT, S], F32, A + 16 * KB)
    QKhi, QKhi_f = both("qk_hi", [P, 2 * DT, S], A + 24 * KB)
    C = top[0]
    hidC_hi, hidC_hif = both("hidC_hi", [P, HT, S])
    hidC_full = place("hidC_full", [P, HT, S], F32, top[0])
    hidC_lo, hidC_lof = both("hidC_lo", [P, HT, S])
    X2hi, X2hif = both("x2T_hi", [P, DT, S], C)
    X2lo, X2lof = both("x2T_lo", [P, DT, S], C + 4 * KB)
    SIL = place("gate", [P, 2, S], F32, C + 8 * KB)
    PT = place("probsT", [P, RING, QUAD, S], F32, C)
    SQ = place("qk_squares", [P, 2 * DT, S], F32, C + 24 * KB)
    RAW = [place(f"raw_weights{n}", [P, PIECE], F32, at) for n, at in enumerate(
        (C, C + 4 * KB, C + 8 * KB, C + 12 * KB, A, A + 4 * KB))]
    ABS = place("raw_weights_lost", [P, 2, PIECE], F32, C + 16 * KB)

    XT = place("xT_sb", [P, DT, S], F32)
    ZB = place("z_blocks", [P, HD, 2 * HD], F32)
    ST, ST_f = both("stacks", [ROWS, 2, QUAD, 2, S])
    VXT = place("v_ones", [P, QT, VX], F32)
    X = place("x_tok", [P, QT, D], F32)
    Vm = place("v_negative", [P, QT, D], F32, top[0])
    T1 = place("scaled_y", [P, QT, D], F32, top[0])
    OUT = place("out_tok", [P, QT, D], F32)
    GAM = place("gamma_b", [P, D], F32)
    BET = place("beta_b", [P, D], F32)
    BV = place("bv_b", [P, D], F32)
    S3 = place("s3_b", [P, D], F32)
    ID = place("ident_sb", [P, P], F32)
    MASK = place("mask", [P, P], F32)
    ONE = place("ones_col", [P, 32], F32)
    WB = place("w_chunk", [P, 2, S], F32)
    BQK = place("bqk", [P, 2 * DT], F32)
    SC = place("scales", [P, 4, HT], F32)
    NEGM = place("neg_max", [P, 2, P], F32)
    MROW, MROW_f = both("max_rows", [MAXES, 2, 2, P])
    QSUM = place("qk_square_sums", [P, 2 * DT], F32)
    QSUM1 = place("qk_square_sum", [P, 1], F32)
    TABLE = place("table_loads", [P, 2], F32)
    GRANT = place("guard_skipped", [P, STEPS + 1], F32)
    REC = place("rec", [P, HD], F32)
    STAT = place("stats", [P, QT, 6], F32)
    MV = place("mean_var", [P, QT, 2], F32)
    NV = place("neg_half_var", [P, QT], F32)
    NY = place("rstd", [P, QT], F32)
    NY_i = NY[:].bitcast(I32)
    NT = place("newton_tmp", [P, QT], F32)
    LOST = place("lost", [P, 32], F32)
    LOST1 = place("lost_row", [P, 1], F32)
    ONESF = place("ones_f", [P, 1], F32)
    FLAG = place("inexact", [1, 1], I32)
    BOUNDED = place("scores_bounded", [1, 1], I32)
    assert top[0] <= nc.sbuf_usable_end, top[0] - nc.sbuf_usable_end

    qk_rows = nc.dram_tensor("qk_rows", [4, D, 2, S], F32, kind="Internal").ap()
    max_rows = nc.dram_tensor("max_rows_d", [2, H * QT * P], F32, kind="Internal").ap()

    with ExitStack() as ctx:
        PS = ctx.enter_context(nc.psum_tensor("PS", [P, 8, 512], F32))

        def sem(name):
            return ctx.enter_context(nc.semaphore(name))

        consts_in, qk_w_in, v_w_in, bqk_in = sem("consts_in"), sem("qk_w_in"), sem("v_w_in"), sem("bqk_in")
        piece_in = [sem(f"piece_in{n}") for n in range(STAGES)]
        xT_in, x_in = sem("xT_in"), sem("x_in")
        stack_in = [sem("stack_in0"), sem("stack_in1")]
        chunk_in = [sem("chunk_in0"), sem("chunk_in1")]
        rows_stored, max_stored, out_stored = sem("rows_stored"), sem("max_stored"), sem("out_stored")
        consts_set, masks_set = sem("consts_set"), sem("masks_set")
        w_rounded, lost, lost_summed = sem("w_rounded"), sem("lost"), sem("lost_summed")
        lost_row_summed, lost_all_summed = sem("lost_row_summed"), sem("lost_all_summed")
        flag_set = sem("flag_set")
        qk_proj, v_proj = sem("qk_proj"), sem("v_proj")
        qk_biased = sem("qk_biased")
        qk_split = sem("qk_split")
        squared, squares_summed = sem("squared"), sem("squares_summed")
        range_known = sem("range_known")
        v_taken, v_step, v_ready = sem("v_taken"), sem("v_step"), sem("v_ready")
        scored = sem("scored")
        maxed = sem("maxed")
        max_turned = sem("max_turned")
        max_hi_done, max_split = sem("max_hi_done"), sem("max_split")
        scoredT = sem("scoredT")
        exp_done = sem("exp_done")
        probs_ready = sem("probs_ready")
        diag_ready = sem("diag_ready")
        pv_done = sem("pv_done")
        zT_taken = sem("zT_taken")
        rec_done, z_taken = sem("rec_done"), sem("z_taken")
        norm_step, last_step = sem("norm_step"), sem("last_step")
        beta_added = sem("beta_added")
        x2_ready, x2_turned = sem("x2_ready"), sem("x2_turned")
        x2_hi_done, x2_split = sem("x2_hi_done"), sem("x2_split")
        ffn1, ffn23 = sem("ffn1"), sem("ffn23")
        gate_done, up_done, gelu_done = sem("gate_done"), sem("up_done"), sem("gelu_done")
        hi_done, lo_done = sem("hi_done"), sem("lo_done")
        y_done, y_taken, out_ready = sem("y_done"), sem("y_taken"), sem("out_ready")
        chunk_used = sem("chunk_used")
        block = ctx.enter_context(nc.Block())

        def per_batch(engine, body):
            body(0, True, False)
            with engine.Fori(1, B - 1) as b:
                body(b, False, False)
            body(B - 1, False, True)

        def after(engine, s, b, n, count):
            value = n * b + count
            if isinstance(value, int) and value <= 0:
                return
            engine.wait_ge(s, value)

        LOADS_S, LOADS_T = 16, 32
        IN_PER_BATCH = 2 * LOADS_S + 2 * LOADS_T

        def after_stack(engine, b, group, transposed):
            had = (2 * LOADS_S + (group // 2) * LOADS_T + LOADS_T) if transposed else (group // 2 + 1) * LOADS_S
            after(engine, stack_in[group % 2], b, IN_PER_BATCH, had)

        def pairs_beside(layer, m, half):
            n = ((layer - 2) * HT + m) * 2 + half
            return [n + 1] * (n + 1 < PAIRS) if n else [0, 1]

        TURNS = {(3, 0, 0): 0, (3, HT - 1, 1): 1}

        def bank1(m, which):
            return 4 + (2 * m + 2 + which) % 4

        def bank23(m):
            return 4 + (m + 2) % 4

        def bank_qk(n):
            return (6, 7, 0, 1)[n]

        START_BANKS = (0, 2, 6)

        CHUNKS = 2 * HT + 2 * 2 * HT + QT * 4

        def x2_part(part):
            if part == 0:
                return PS[:, 4:4 + DT, 0:X2_CUT], slice(0, X2_CUT)
            return PS[:, 6, 0:DT * P].rearrange("p (c s) -> p c s", c=DT), slice(X2_CUT, S)

        PIECES = [(src, w, k, PIECE // w.shape[2])
                  for src, w in ((w1T, W1), (w2T, W2), (h1T, G1), (h2T, G2), (w3T, W3))
                  for k in range(0, w.shape[1], PIECE // w.shape[2])]
        N_CONSTS = 6

        @block.sync
        def _(sp):
            sp.dma_start(XT[:], xT[0:D, :].rearrange("(t p) s -> p t s", p=P)).then_inc(xT_in, 16)
            sp.dma_start(WK[:], wkT.rearrange("(t p) m -> p t m", p=P)).then_inc(qk_w_in, 16)
            sp.dma_start(WV[:], wvT.rearrange("(t p) m -> p t m", p=P)).then_inc(v_w_in, 16)
            sp.dma_start(SC[:], scales.rearrange("p (n t) -> p n t", n=4)).then_inc(consts_in, 16)
            sp.dma_start(BV[:], bv.rearrange("(a d) -> a d", a=1).to_broadcast([P, D])).then_inc(consts_in, 16)
            sp.dma_start(ID[:], ident).then_inc(consts_in, 16)
            for t, src in ((GAM, gamma), (BET, beta), (S3, s3)):
                sp.dma_start(t[:], src.rearrange("(a d) -> a d", a=1).to_broadcast([P, D])).then_inc(consts_in, 16)

            def load_stacks(b, group, transposed):
                n, back = 2 * H, 2 * QUAD * (group - 1)
                if group >= 2:
                    after(sp, scoredT if transposed else scored, b, n, back)
                else:
                    after(sp, scored if transposed else scoredT, b, n, back + n - (0 if transposed else n))
                if group == 0 and not transposed:
                    after(sp, rows_stored, b, 8 * 16, 8 * 16)
                rows = qk_rows.rearrange("r (d h) a s -> (r d) h a s", d=HD)
                sp.dma_start(ST_f[0:SPLIT, group % 2, :, :, :],
                             rows[:, group * QUAD:(group + 1) * QUAD, :, :]).then_inc(stack_in[group % 2], 16)
                if transposed:
                    if group % 2 == 0:
                        after(sp, max_stored, b, 32, 16 * (group // 2 + 1))
                    sp.dma_start(ST_f[SPLIT:ROWS, group % 2, :, 0, :],
                                 max_rows[:, group * QUAD * S:(group + 1) * QUAD * S].rearrange(
                                     "r (h s) -> r h s", h=QUAD)).then_inc(stack_in[group % 2], 16)

            def store_rows(b):
                for part, done, products in ((QKhi_f, qk_biased, ((0, 1), (0, 2))), (QKlo_f, qk_split, ((2, 3), (1, 3)))):
                    for a in range(2):
                        after(sp, done, b, 2 * DT, (a + 1) * DT)
                        for r in products[a]:
                            sp.dma_start(qk_rows[r, :, a, :].rearrange("(t p) s -> p t s", p=P),
                                         part[:, a * DT:(a + 1) * DT, :]).then_inc(rows_stored, 16)

            def chunks(b, first, count, source):
                for c in range(first, first + count):
                    after(sp, chunk_used, b, CHUNKS, c - 1)
                    src, shape = source(c - first)
                    sp.dma_start(WB[:, c % 2, 0:shape[0] * shape[1]].rearrange("p (k m) -> p k m", m=shape[1]),
                                 src).then_inc(chunk_in[c % 2], 16)

            def store_max(b, half):
                after(sp, max_split, b, 2, half + 1)
                sp.dma_start(max_rows[:, half * MAXES * P:(half + 1) * MAXES * P].rearrange("r (q p) -> q r p", p=P),
                             MROW_f[:, half, :, :]).then_inc(max_stored, 16)

            def start_attention(b):
                store_max(b, 0)
                load_stacks(b, 0, True)
                store_max(b, 1)

            def feed_forward(b, last, general):
                def hidden(src, m):
                    return lambda c: (src.rearrange("(k p) m -> p k m", p=P)[:, 4 * c:4 * c + 4, m * P:(m + 1) * P], (4, P))

                def head_group(g):
                    if not last:
                        load_stacks(b + 1, g, False)

                if not general:
                    if not last:
                        for g in range(NQUAD):
                            load_stacks(b + 1, g, False)
                        start_attention(b + 1)
                    return
                head_group(0)
                head_group(1)
                c0 = 0
                for m in range(HT):
                    for w in (w1T, w2T):
                        chunks(b, c0, 1, lambda c: (w.rearrange("(k p) m -> p k m", p=P)[:, :, m * P:(m + 1) * P], (DT, P)))
                        c0 += 1
                for layer, w in ((2, h1T), (3, h2T)):
                    for m in range(HT):
                        if (layer, m) == (2, 4):
                            head_group(2)
                        if (layer, m) == (3, 0):
                            head_group(3)
                        chunks(b, c0, 2, hidden(w, m))
                        c0 += 2
                if not last:
                    start_attention(b + 1)
                for t in range(QT):
                    chunks(b, c0, 4, lambda c: (w3T.rearrange("(k p) m -> p k m", p=P)[:, 2 * c:2 * c + 2, :], (2, D)))
                    c0 += 4

            store_rows(0)
            for g in range(NQUAD):
                load_stacks(0, g, False)
            start_attention(0)
            inexact = []

            def body(b, first, last):
                here = b * S if isinstance(b, int) else sp.snap(b * S)
                before = (b - 1) * S if isinstance(b, int) else sp.snap((b - 1) * S)
                next_dims = (b + 1) * D if isinstance(b, int) else sp.snap((b + 1) * D)
                if not last:
                    after(sp, v_proj, b, QT, QT)
                    sp.dma_start(XT[:], xT[bass.ds(next_dims, D), :].rearrange("(t p) s -> p t s", p=P)).then_inc(xT_in, 16)
                load_stacks(b, 1, True)
                load_stacks(b, 2, True)
                after(sp, out_ready, b, QT, 0)
                sp.dma_start(X[:], x[bass.ds(here, S), :].rearrange("(t p) d -> p t d", p=P)).then_inc(x_in, 16)
                if not first:
                    sp.dma_start(out[bass.ds(before, S), :].rearrange("(t p) d -> p t d", p=P), OUT[:]).then_inc(out_stored, 16)
                load_stacks(b, 3, True)
                if not last:
                    store_rows(b + 1)
                if first:
                    sp.wait_ge(flag_set, 1)
                    inexact.append(sp.value_load(FLAG[0:1, 0:1], min_val=0, max_val=1))
                with sp.If(inexact[0]):
                    feed_forward(b, last, True)
                if not last:
                    with sp.Else():
                        feed_forward(b, last, False)

            per_batch(sp, body)
            sp.wait_ge(out_ready, QT * B)
            sp.dma_start(out[(B - 1) * S:B * S, :].rearrange("(t p) d -> p t d", p=P), OUT[:]).then_inc(out_stored, 16)
            sp.wait_ge(out_stored, 16 * B)
            sp.wait_ge(rows_stored, 8 * 16 * B)
            sp.wait_ge(max_stored, 2 * 16 * B)

        @block.gpsimd
        def _(pool):
            nc.gpsimd.memset(MASK[:], 1.0).then_inc(masks_set, 1)
            nc.gpsimd.memset(ONE[:], 0.0).then_inc(masks_set, 1)
            pool.wait_ge(masks_set, 2)
            nc.gpsimd.affine_select(out=MASK[:], in_=MASK[:], compare_op=ALU.is_ge, fill=0.0, base=0,
                                    pattern=[[-1, P]], channel_multiplier=1).then_inc(masks_set, 1)
            nc.gpsimd.memset(ONE[:, HD:HD + 1], 1.0).then_inc(masks_set, 1)

            def low_part(n_before, b, full, hi, lo, m):
                after(pool, hi_done, b, 3 * HT, n_before + m + 1)
                nc.gpsimd.tensor_tensor(lo[:, m, :], full[:, m, :], hi[:, m, :], ALU.subtract).then_inc(lo_done, 1)

            def masks(b, s):
                kt = s % QT
                if s == 0:
                    after(pool, y_done, b, QT, 0)
                after(pool, probs_ready, b, 2 * STEPS, 2 * s + 2)
                after(pool, pv_done, b, STEPS, s - 1)
                nc.gpsimd.tensor_tensor(PM[:, s % 2, :, :], PT[:, s % RING, :, kt * P:(kt + 1) * P],
                                        MASK[:].rearrange("p (a m) -> p a m", a=1).to_broadcast([P, QUAD, P]),
                                        ALU.mult).then_inc(diag_ready, 1)

            def split_qk(b):
                for n in range(2 * DT):
                    after(pool, qk_biased, b, 2 * DT, n + 1)
                    nc.gpsimd.tensor_tensor(QKlo[:, n, :], QKf[:, n, :], QKhi_f[:, n, :],
                                            ALU.subtract).then_inc(qk_split, 1)

            def body(b, first, last):
                for s in range(STEPS):
                    masks(b, s)
                    if s == X_AT:
                        after(pool, x_in, b, 16, 16)
                        nc.gpsimd.tensor_tensor(XB[:], X[:], BET[:].rearrange("p (a d) -> p a d", a=1).to_broadcast(
                            [P, QT, D]), ALU.add).then_inc(beta_added, 1)
                if not last:
                    split_qk(b + 1)
                for m in range(HT):
                    low_part(0, b, hidA_full, hidA_hif, hidA_lo, m)
                for m in range(HT):
                    low_part(HT, b, hidC_full, hidC_hif, hidC_lo, m)
                for m in range(HT):
                    low_part(2 * HT, b, hidA_full, hidA_hif, hidA_lo, m)

            split_qk(0)
            for n in range(len(PIECES)):
                _, w, k, kts = PIECES[n]
                raw = RAW[n % STAGES][:].rearrange("p (k m) -> p k m", k=kts)
                pool.wait_ge(w_rounded, n + 1)
                nc.gpsimd.tensor_tensor(raw, raw, w[:, k:k + kts, :].bitcast(F32), ALU.subtract).then_inc(lost, 1)
            pool.wait_ge(consts_in, 16 * N_CONSTS)
            per_batch(pool, body)

        @block.scalar
        def _(act):
            def take_x2_hi(b, part):
                after(act, x2_turned, b, 2, part + 1)
                src, dst = x2_part(part)
                nc.scalar.activation(X2hi[:, :, dst], src, ACT.Identity).then_inc(x2_hi_done, 1)

            def bias_qk(b, parts):
                for n in parts:
                    after(act, qk_proj, b, 2 * DT, n + 1)
                    nc.scalar.activation(QKf[:, n, :], PS[:, bank_qk(n), :], ACT.Identity,
                                         bias=BQK[:, n:n + 1])
                    nc.scalar.activation(QKhi[:, n, :], PS[:, bank_qk(n), :], ACT.Identity,
                                         bias=BQK[:, n:n + 1]).then_inc(qk_biased, 1)

            def square_qk(b, n):
                after(act, qk_biased, b, 2 * DT, n + 1)
                nc.scalar.activation(SQ[:, n, :], QKhi_f[:, n, :], ACT.Square,
                                     accum_out=QSUM[:, n:n + 1]).then_inc(squared, 1)

            def load_piece(n):
                src, w, k, kts = PIECES[n]
                act.dma_start(RAW[n % STAGES][:].rearrange("p (k m) -> p k m", k=kts),
                              src.rearrange("(k p) m -> p k m", p=P)[:, k:k + kts, :]).then_inc(piece_in[n % STAGES], 16)

            def round_piece(n):
                _, w, k, kts = PIECES[n]
                act.wait_ge(piece_in[n % STAGES], 16 * (n // STAGES + 1))
                nc.scalar.activation(w[:, k:k + kts, :], RAW[n % STAGES][:].rearrange("p (k m) -> p k m", k=kts),
                                     ACT.Identity).then_inc(w_rounded, 1)

            def sum_lost(n):
                act.wait_ge(lost, n + 1)
                if n >= 2:
                    act.wait_ge(lost_summed, n - 1)
                nc.scalar.activation(ABS[:, n % 2, :], RAW[n % STAGES][:], ACT.Abs,
                                     accum_out=LOST[:, n:n + 1]).then_inc(lost_summed, 1)

            def body(b, first, last):
                for s in range(STEPS):
                    for pair in range(2):
                        after(act, scoredT, b, 2 * STEPS, 2 * s + pair + 1)
                        if s >= RING:
                            after(act, pv_done, b, STEPS, s - RING + 1)
                        nc.scalar.activation(PT[:, s % RING, 2 * pair:2 * pair + 2, :],
                                             PS[:, 2 * pair:2 * pair + 2, :], ACT.Exp,
                                             scale=SCALE).then_inc(exp_done, 1)
                if not last:
                    bias_qk(b + 1, range(DT))
                take_x2_hi(b, 0)
                if not last:
                    bias_qk(b + 1, range(DT, 2 * DT))
                take_x2_hi(b, 1)
                nc.scalar.activation(TABLE[:, 0:1], ONESF[:], ACT.Silu)
                for m in range(HT):
                    after(act, ffn1, b, 2 * HT, 2 * m + 1)
                    if m >= 2:
                        after(act, up_done, b, HT, m - 1)
                    nc.scalar.activation(SIL[:, m % 2, :], PS[:, bank1(m, 0), :], ACT.Silu,
                                         scale=SC[:, 0, m:m + 1]).then_inc(gate_done, 1)
                    if m < 2 * DT and not last:
                        square_qk(b + 1, m)
                for layer, full in ((2, hidC_full), (3, hidA_full)):
                    for m in range(HT):
                        after(act, ffn23, b, 2 * HT, (layer - 2) * HT + m + 1)
                        nc.scalar.activation(full[:, m, :], PS[:, bank23(m), :], ACT.Gelu,
                                             scale=SC[:, layer, m:m + 1]).then_inc(gelu_done, 1)
                if not last:
                    nc.scalar.activation(TABLE[:, 1:2], ONESF[:], ACT.Exp)

            act.wait_ge(consts_set, 1)
            nc.scalar.activation(TABLE[:, 0:1], ONESF[:], ACT.Identity)
            act.dma_start(WQ[:], wqT.rearrange("(t p) m -> p t m", p=P)).then_inc(qk_w_in, 16)
            act.dma_start(BQK[:], bqk).then_inc(bqk_in, 16)
            for n in range(STAGES):
                load_piece(n)
            act.wait_ge(bqk_in, 16)
            bias_qk(0, range(2 * DT))
            for n in range(2 * DT):
                square_qk(0, n)
            act.wait_ge(consts_in, 16 * N_CONSTS)
            for n in range(len(PIECES) + BEHIND):
                if n < len(PIECES):
                    round_piece(n)
                if n >= BEHIND:
                    sum_lost(n - BEHIND)
                if 0 <= n - BEHIND < len(PIECES) - STAGES:
                    act.wait_ge(lost_summed, n - BEHIND + 1)
                    load_piece(n - BEHIND + STAGES)
            act.wait_ge(lost_summed, len(PIECES))
            per_batch(act, body)

        @block.vector
        def _(dve):
            nc.vector.memset(ONESF[:], 1.0).then_inc(consts_set, 1)
            nc.vector.memset(ST_f[SPLIT:ROWS, :, :, 1, :], 1.0).then_inc(consts_set, 1)
            nc.vector.memset(VXT[:], 1.0).then_inc(consts_set, 1)
            nc.vector.memset(NEGM[:], 0.0).then_inc(consts_set, 1)

            def take_v(b):
                after(dve, v_proj, b, QT, QT)
                after(dve, pv_done, b, STEPS, 0)
                nc.vector.tensor_tensor(
                    v_part(slice(0, QT)),
                    PS[:, 2:4, :].rearrange("p a (t h e) -> p (a t) h e", t=2, e=HD),
                    BV[:].rearrange("p (a h e) -> p a h e", a=1, e=HD).to_broadcast([P, QT, H, HD]),
                    ALU.add).then_inc(v_taken, 1)

            def v_part(t):
                return VXT[:, t, 0:H * VW].rearrange("p t (h e) -> p t h e", e=VW)[:, :, :, 0:HD]

            def guard_v(b, t):
                after(dve, v_taken, b, 1, 1)
                if t == 0:
                    after(dve, out_stored, b, 16, -16)
                v, negative = v_part(slice(t, t + 1)), Vm[:, t:t + 1, :].rearrange("p t (h e) -> p t h e", e=HD)
                nc.vector.tensor_scalar(negative, v, 0.0, None, ALU.min).then_inc(v_step, 1)
                after(dve, v_step, b, QT, t + 1)
                nc.vector.scalar_tensor_tensor(out=v, in0=v, scalar=0.0, in1=negative,
                                               op0=ALU.max, op1=ALU.add).then_inc(v_ready, 1)

            def row_max(b, pair, bank=None):
                h, half = divmod(pair, 2)
                bank = 2 * half if bank is None else bank
                after(dve, scored, b, PAIRS, pair + 1)
                at = h % (H // 2) * QT + 2 * half
                nc.vector.tensor_reduce(NEGM[:, h // (H // 2), at:at + 2],
                                        PS[:, bank:bank + 2, :], AX.X, ALU.max,
                                        negate=True).then_inc(maxed, 1)

            def sum_squares(b):
                after(dve, squared, b, 2 * DT, 2 * DT)
                nc.vector.tensor_reduce(QSUM1[:], QSUM[:], AX.X, ALU.add).then_inc(squares_summed, 1)

            def split_max(b, half):
                after(dve, max_turned, b, 2, half + 1)
                after(dve, max_stored, b, 32, 0)
                nc.vector.tensor_copy(MROW[:, half, 0, :], PS[0:MAXES, 0, 0:P]).then_inc(max_hi_done, 1)
                if half == 0:
                    nc.vector.tensor_scalar(BOUNDED[:], PS[0:1, 0, P:P + 1], SAFE_SQUARES, None,
                                            ALU.is_le).then_inc(range_known, 1)
                after(dve, max_hi_done, b, 2, half + 1)
                nc.vector.tensor_tensor(MROW[:, half, 1, :], PS[0:MAXES, 0, 0:P], MROW_f[:, half, 0, :],
                                        ALU.subtract).then_inc(max_split, 1)

            def guard(b, s, bounded):
                if bounded:
                    after(dve, exp_done, b, 2 * STEPS, 2 * s + 2)
                    nc.vector.memset(GRANT[:, s:s + 1], 0.0).then_inc(probs_ready, 2)
                    return
                for pair in range(2):
                    after(dve, exp_done, b, 2 * STEPS, 2 * s + pair + 1)
                    p = PT[:, s % RING, 2 * pair:2 * pair + 2, :]
                    nc.vector.tensor_scalar(p, p, 0.0, None, ALU.max).then_inc(probs_ready, 1)

            def take_z(b, g):
                after(dve, pv_done, b, STEPS, QT * (g + 1))
                nc.vector.transpose(ZB[:], PS[:, 4 + g % 2, :].rearrange("p (r c) -> p c r", c=HD)).then_inc(zT_taken, 1)
                after(dve, zT_taken, b, NQUAD, g + 1)
                nc.vector.tensor_scalar(REC[:].rearrange("p (c e) -> p c e", e=1), ZB[:, :, HD:HD + 1], TINY, None,
                                        ALU.max).then_inc(rec_done, 1)
                after(dve, rec_done, b, 2 * NQUAD, 2 * g + 1)
                nc.vector.reciprocal(REC[:], REC[:]).then_inc(rec_done, 1)
                after(dve, rec_done, b, 2 * NQUAD, 2 * g + 2)
                nc.vector.tensor_tensor(
                    Z[:, g, :].rearrange("p (c e) -> p c e", e=HD), ZB[:, :, 0:HD],
                    REC[:].rearrange("p (c e) -> p c e", e=1).to_broadcast([P, HD, HD]), ALU.mult).then_inc(z_taken, 1)

            def rstd(tiles, step, b, n, count, meanwhile=None):
                done = [count]
                y, nv, t = NY[:, tiles], NV[:, tiles], NT[:, tiles]
                one = tiles.stop - tiles.start == 1

                def then(ins, wait=True):
                    done[0] += 1
                    ins.then_inc(step, 1)
                    if wait:
                        after(dve, step, b, n, done[0])

                then(nc.vector.tensor_scalar(y, MV[:, tiles, 1], EPS, None, ALU.add))
                then(nc.vector.tensor_scalar(nv, y, -0.5, None, ALU.mult), False)
                then(nc.vector.tensor_scalar(NY_i[:, tiles], NY_i[:, tiles], -0.5, RSQRT_SEED, ALU.mult, ALU.add), False)
                if meanwhile is not None:
                    then(meanwhile(), False)
                after(dve, step, b, n, done[0])
                for _ in range(NEWTON):
                    if one:
                        then(nc.vector.scalar_tensor_tensor(out=t, in0=y, scalar=nv, in1=y,
                                                            op0=ALU.mult, op1=ALU.mult))
                    else:
                        then(nc.vector.tensor_tensor(t, y, y, ALU.mult))
                        then(nc.vector.tensor_tensor(t, t, nv, ALU.mult))
                    then(nc.vector.scalar_tensor_tensor(out=y, in0=t, scalar=1.5, in1=y,
                                                        op0=ALU.add, op1=ALU.mult))
                return done[0]

            def normalize(src, dst, t):
                return nc.vector.tensor_scalar(dst[:, t, :], src[:, t, :], MV[:, t, 0:1], NY[:, t:t + 1],
                                               ALU.subtract, ALU.mult)

            RS1, RS = 3 + 2 * NEWTON, 3 + 3 * NEWTON
            N_NORM = 2 + RS1
            N_TILE = 2 * N_NORM + 3
            N12 = QT * N_TILE

            def norm_steps(b, count):
                n = [count]

                def then(ins, wait=True):
                    n[0] += 1
                    ins.then_inc(norm_step, 1)
                    if wait:
                        after(dve, norm_step, b, N12, n[0])

                return n, then

            def statistics(src, t, b, n, then, meanwhile=None):
                then(nc.vector.bn_stats(STAT[:, t, :], src[:, t, :]))
                nc.vector.memset(NT[:, t:t + 1], 0.0)
                then(nc.vector.bn_aggr(MV[:, t, :], STAT[:, t, :]))
                n[0] = rstd(slice(t, t + 1), norm_step, b, N12, n[0], meanwhile)

            def first_norm(b, t):
                n, then = norm_steps(b, t * N_TILE)
                after(dve, z_taken, b, NQUAD, t + 1)
                if t == 0:
                    after(dve, x_in, b, 16, 16)
                then(nc.vector.tensor_tensor(Z[:, t, :], Z[:, t, :], X[:, t, :], ALU.add))
                statistics(Z, t, b, n, then, lambda: nc.vector.scalar_tensor_tensor(
                    out=Z[:, t, :], in0=Z[:, t, :], scalar=MV[:, t, 0:1], in1=GAM[:], op0=ALU.subtract, op1=ALU.mult))
                if t == 0:
                    after(dve, beta_added, b, 1, 1)
                then(nc.vector.scalar_tensor_tensor(out=X[:, t, :], in0=Z[:, t, :], scalar=NY[:, t:t + 1],
                                                    in1=XB[:, t, :], op0=ALU.mult, op1=ALU.add), False)
                assert n[0] == t * N_TILE + N_TILE - N_NORM

            def second_norm(b, t):
                n, then = norm_steps(b, t * N_TILE + N_TILE - N_NORM)
                after(dve, norm_step, b, N12, n[0])
                statistics(X, t, b, n, then)
                assert n[0] == (t + 1) * N_TILE
                normalize(X, X, t).then_inc(x2_ready, 1)

            def split_x2(b):
                for part in range(2):
                    after(dve, x2_hi_done, b, 2, part + 1)
                    src, dst = x2_part(part)
                    nc.vector.tensor_tensor(X2lo[:, :, dst], src, X2hif[:, :, dst], ALU.subtract).then_inc(x2_split, 1)

            N_LAST = 3 * QT + RS

            def add_y(b, tiles, back=0):
                for t in tiles:
                    if t == 0:
                        after(dve, x2_ready, b, QT, QT)
                        after(dve, out_stored, b, 16, 0)
                    after(dve, y_done, b, QT, t + 1 - QT * back)
                    nc.vector.tensor_tensor(T1[:, t, :], PS[:, bank23(t), 0:D], S3[:], ALU.mult).then_inc(y_taken, 1)
                    after(dve, y_taken, b, QT, t + 1 - QT * back)
                    nc.vector.tensor_tensor(X[:, t, :], X[:, t, :], T1[:, t, :], ALU.add).then_inc(last_step, 1)
                    after(dve, last_step, b, N_LAST, 2 * t + 1 - N_LAST * back)
                    nc.vector.bn_stats(STAT[:, t, :], X[:, t, :]).then_inc(last_step, 1)

            def last_norm(b, parts=range(3)):
                if 0 in parts:
                    add_y(b, (QT - 1,), 1)
                if 1 in parts:
                    after(dve, last_step, b, N_LAST, 2 * QT - N_LAST)
                    nc.vector.memset(NT[:, 0:1], 0.0)
                    for t in range(QT):
                        nc.vector.bn_aggr(MV[:, t, :], STAT[:, t, :]).then_inc(last_step, 1)
                    after(dve, last_step, b, N_LAST, 3 * QT - N_LAST)
                    rstd(slice(0, QT), last_step, b, N_LAST, 3 * QT - N_LAST)
                if 2 in parts:
                    for t in range(QT):
                        normalize(X, OUT, t).then_inc(out_ready, 1)

            def attention(b, first, bounded):
                for s in range(STEPS):
                    guard(b, s, bounded)
                    if LAG - 1 <= s < LAG + 2 and not first:
                        last_norm(b, (s - LAG + 1,))
                    g, ago = divmod(s - (QT - 1 + LAG), QT)
                    if ago == 0 and g >= 0:
                        take_z(b, g)
                    if ago == 1 and g >= 0:
                        first_norm(b, g)
                    if ago == 2 and g >= 0:
                        second_norm(b, g)
                for g in range(NQUAD):
                    last_ago = STEPS - 1 - (QT - 1 + LAG) - QT * g
                    if last_ago < 0:
                        take_z(b, g)
                    if last_ago < 1:
                        first_norm(b, g)
                    if last_ago < 2:
                        second_norm(b, g)

            def body(b, first, last):
                after(dve, range_known, b, 1, 1)
                nc.vector.memset(GRANT[:, STEPS:], 0.0)
                bounded = dve.value_load(BOUNDED[0:1, 0:1], min_val=0, max_val=1)
                with dve.If(bounded):
                    attention(b, first, True)
                with dve.Else():
                    attention(b, first, False)
                split_x2(b)
                if not last:
                    take_v(b + 1)
                for m in range(HT):
                    after(dve, gate_done, b, HT, m + 1)
                    after(dve, ffn1, b, 2 * HT, 2 * m + 2)
                    if m == 0 and not last:
                        after(dve, qk_split, b, 2 * DT, 4 * DT)
                    if m == 4 and not last:
                        sum_squares(b + 1)
                        after(dve, rows_stored, b, 8 * 16, 16 * 16)
                    nc.vector.scalar_tensor_tensor(out=hidA_full[:, m, :], in0=PS[:, bank1(m, 1), :],
                                                   scalar=SC[:, 1, m:m + 1], in1=SIL[:, m % 2, :],
                                                   op0=ALU.mult, op1=ALU.mult).then_inc(up_done, 1)
                    after(dve, up_done, b, HT, m + 1)
                    nc.vector.tensor_copy(hidA_hi[:, m, :], hidA_full[:, m, :]).then_inc(hi_done, 1)
                for layer, full, hi in ((2, hidC_full, hidC_hi), (3, hidA_full, hidA_hi)):
                    for m in range(HT):
                        if not last:
                            for half in range(2):
                                if (layer, m, half) in TURNS:
                                    split_max(b + 1, TURNS[layer, m, half])
                                for pair in pairs_beside(layer, m, half):
                                    row_max(b + 1, pair)
                        after(dve, gelu_done, b, 2 * HT, (layer - 2) * HT + m + 1)
                        nc.vector.tensor_copy(hi[:, m, :], full[:, m, :]).then_inc(hi_done, 1)
                        if not last and layer == 2 and m < QT:
                            guard_v(b + 1, m)
                add_y(b, range(QT - 1))
                if last:
                    last_norm(B)

            dve.wait_ge(consts_in, 16 * N_CONSTS)
            dve.wait_ge(consts_set, 4)
            take_v(0)
            for t in range(QT):
                guard_v(0, t)
            sum_squares(0)
            for half in range(2):
                for pair in range(half * H, half * H + H):
                    row_max(0, pair, START_BANKS[pair % 3])
                split_max(0, half)
            dve.wait_ge(lost_summed, len(PIECES))
            nc.vector.tensor_reduce(LOST1[:], LOST[:, 0:len(PIECES)], AX.X, ALU.add).then_inc(lost_row_summed, 1)
            dve.wait_ge(lost_all_summed, 1)
            nc.vector.tensor_scalar(FLAG[:], PS[0:1, 7, 0:1], 0.0, None, ALU.not_equal).then_inc(flag_set, 1)
            per_batch(dve, body)

        @block.tensor
        def _(pe):
            def project(b, parts):
                after(pe, xT_in, b, 16, 16)
                for n in parts:
                    if n == 0:
                        after(pe, y_taken, b, QT, -QT)
                    if n == DT:
                        after(pe, exp_done, b, 2 * STEPS, 0)
                    w, c = (WQ, WK)[n // DT], n % DT
                    for k in range(DT):
                        ins = nc.tensor.matmul(PS[:, bank_qk(n), :], w[:, k, c * P:(c + 1) * P], XT[:, k, :],
                                               start=(k == 0), stop=(k == DT - 1))
                    ins.then_inc(qk_proj, 1)

            def project_v(b, tiles):
                if isinstance(b, int) and b == 0:
                    pe.wait_ge(v_w_in, 16)
                for t in tiles:
                    for k in range(DT):
                        ins = nc.tensor.matmul(PS[:, 2 + t // 2, t % 2 * D:(t % 2 + 1) * D],
                                               XT[:, k, t * P:(t + 1) * P], WV[:, k, :],
                                               start=(k == 0), stop=(k == DT - 1))
                    ins.then_inc(v_proj, 1)

            def row_scores(b, pair, behind_turn=False, banks=(0, 2)):
                h, half = divmod(pair, 2)
                if h % QUAD == 0 and half == 0:
                    after_stack(pe, b, h // QUAD, False)
                if pair == 0:
                    after(pe, qk_biased, b, 2 * DT, 2 * DT)
                elif pair == 1:
                    after(pe, v_taken, b, 1, 1)
                elif pair >= len(banks):
                    after(pe, maxed, b, PAIRS, pair - len(banks) + 1)
                if behind_turn:
                    after(pe, max_split, b, 2, 1)
                for n, qt in enumerate((2 * half, 2 * half + 1)):
                    ins = nc.tensor.matmul(PS[:, banks[pair % len(banks)] + n, :],
                                           ST[0:SPLIT, (h // QUAD) % 2, h % QUAD, 0, qt * P:(qt + 1) * P],
                                           ST[0:SPLIT, (h // QUAD) % 2, h % QUAD, 1, :],
                                           start=True, stop=True)
                ins.then_inc(scored, 1)

            def keep_warm(bank, products):
                for _ in range(products):
                    nc.tensor.matmul(PS[:, bank, :], W1[:, 0, 0:P], W1[:, 0, 0:512], start=True, stop=True)

            def turn_max(b, half, pairs):
                after(pe, maxed, b, PAIRS, pairs)
                if half == 0:
                    after(pe, squares_summed, b, 1, 1)
                    nc.tensor.matmul(PS[0:1, 0, P:P + 1], QSUM1[:], ONESF[:], start=True, stop=True)
                nc.tensor.transpose(PS[:, 0, 0:P], NEGM[:, half, :], ID[:]).then_inc(max_turned, 1)

            def scores_T(b, s):
                g, kt = divmod(s, QT)
                if kt == 0:
                    after_stack(pe, b, g, True)
                for pair in range(2):
                    if s:
                        after(pe, exp_done, b, 2 * STEPS, 2 * s + pair - 1)
                    else:
                        after(pe, max_split, b, 2, 2)
                        after(pe, maxed, b, PAIRS, PAIRS)
                    for j in (2 * pair, 2 * pair + 1):
                        ins = nc.tensor.matmul(PS[:, j, :], ST[:, g % 2, j, 1, kt * P:(kt + 1) * P],
                                               ST[:, g % 2, j, 0, :], start=True, stop=True)
                    ins.then_inc(scoredT, 1)

            def values(b, s):
                g, kt = divmod(s, QT)
                bank = 4 + g % 2
                if kt == 0:
                    if g < 2:
                        after(pe, y_taken, b, QT, g - 1)
                    else:
                        after(pe, zT_taken, b, NQUAD, g - 1)
                after(pe, probs_ready, b, 2 * STEPS, 2 * s + 2)
                after(pe, v_ready, b, QT, QT)
                lo, hi = kt * P, (kt + 1) * P
                for j in range(QUAD):
                    nc.tensor.matmul(PS[32 * j:32 * j + 32, bank, lo:S], ONE[:, 0:32],
                                     PT[:, s % RING, j, lo:S], start=(kt == 0), stop=False,
                                     skip_group_check=True)
                if kt:
                    for j in range(QUAD):
                        h = g * QUAD + j
                        nc.tensor.matmul(PS[32 * j:32 * j + 32, bank, 0:lo], VXT[:, kt, VW * h:VW * h + 32],
                                         PT[:, s % RING, j, 0:lo], start=False, stop=False,
                                         skip_group_check=True)
                after(pe, diag_ready, b, STEPS, s + 1)
                for j in range(QUAD):
                    h = g * QUAD + j
                    ins = nc.tensor.matmul(PS[32 * j:32 * j + HD, bank, lo:hi], VXT[:, kt, VW * h:VW * h + HD],
                                           PM[:, s % 2, j, :], start=False, stop=(kt == QT - 1),
                                           skip_group_check=True)
                ins.then_inc(pv_done, 1)

            def turn_x2(b, part, last):
                if part == 0:
                    after(pe, zT_taken, b, NQUAD, NQUAD)
                elif not last:
                    after(pe, qk_biased, b, 2 * DT, 2 * DT + 1)
                bank, tokens = x2_part(part)
                for t in range(tokens.start // P, tokens.stop // P):
                    after(pe, x2_ready, b, QT, t + 1)
                    for c in range(DT):
                        at = t * P - tokens.start
                        ins = nc.tensor.transpose(bank[:, c, at:at + P], X[:, t, c * P:(c + 1) * P], ID[:])
                ins.then_inc(x2_turned, 1)

            def feed_forward(b, last, general):
                chunk = [0]

                def beside(layer, m, half):
                    if last:
                        return
                    pairs = pairs_beside(layer, m, half)
                    if (layer, m, half) in TURNS:
                        turn_max(b + 1, TURNS[layer, m, half], pairs[0] if pairs else PAIRS)
                    for pair in pairs:
                        row_scores(b + 1, pair, behind_turn=(layer, m, half) == (3, 0, 1))

                def product(out, kts, weights, data, when, signal, per_chunk, swapped=False, halfway=None):
                    for k in range(kts):
                        if halfway is not None and k == kts // 2:
                            halfway()
                        if when is not None:
                            after(pe, lo_done, b, 3 * HT, when + k + 1)
                        if general and k % per_chunk == 0:
                            c = chunk[0]
                            chunk[0] += 1
                            after(pe, chunk_in[c % 2], b, CHUNKS // 2 * 16, 16 * (c // 2 + 1))
                        for part in (0, 1):
                            d = data(k)[2 * general + part]
                            if general:
                                width = D if swapped else P
                                w = WB[:, c % 2, (k % per_chunk) * width:(k % per_chunk + 1) * width]
                            else:
                                w = weights(k)
                            ins = nc.tensor.matmul(out, d if swapped else w, w if swapped else d,
                                                   start=(k == 0 and part == 0), stop=(k == kts - 1 and part == 1))
                        if general and k % per_chunk == per_chunk - 1 and k < kts - 1:
                            ins.then_inc(chunk_used, 1)
                    ins.then_inc(signal, 1)
                    if general:
                        nc.tensor.drain().then_inc(chunk_used, 1)

                for m in range(HT):
                    for which, w in ((0, W1), (1, W2)):
                        if m == 0:
                            after(pe, x2_split, b, 2, 2)
                            if not last:
                                after(pe, qk_biased, b, 2 * DT, 2 * DT + 2)
                        if m >= 2:
                            after(pe, (gate_done, up_done)[which], b, HT, m - 1)
                        product(PS[:, bank1(m, which), :], DT, lambda k: w[:, k, m * P:(m + 1) * P],
                                lambda k: (X2hi[:, k, :], X2lo[:, k, :], X2hif[:, k, :], X2lof[:, k, :]),
                                None, ffn1, DT)
                for layer, w, (hi, lo, hif, lof) in (
                        (2, G1, (hidA_hi, hidA_lo, hidA_hif, hidA_lof)),
                        (3, G2, (hidC_hi, hidC_lo, hidC_hif, hidC_lof))):
                    for m in range(HT):
                        beside(layer, m, 0)
                        if layer == 2 and m < 4:
                            after(pe, (gate_done, up_done)[m % 2], b, HT, 7 + m // 2)
                        else:
                            after(pe, gelu_done, b, 2 * HT, (layer - 2) * HT + m - 3)
                        product(PS[:, bank23(m), :], HT, lambda k: w[:, k, m * P:(m + 1) * P],
                                lambda k: (hi[:, k, :], lo[:, k, :], hif[:, k, :], lof[:, k, :]),
                                (layer - 2) * HT if m == 0 else None, ffn23, 4,
                                halfway=lambda: beside(layer, m, 1))
                for t in range(QT):
                    if not last and t * LAG % QT == 0:
                        scores_T(b + 1, t * LAG // QT)
                    tok = slice(t * P, (t + 1) * P)
                    after(pe, gelu_done, b, 2 * HT, HT + 5 + t)
                    product(PS[:, bank23(t), 0:D], HT, lambda k: W3[:, k, :],
                            lambda k: (hidA_hi[:, k, tok], hidA_lo[:, k, tok], hidA_hif[:, k, tok], hidA_lof[:, k, tok]),
                            2 * HT if t == 0 else None, y_done, 2, swapped=True)

            pe.wait_ge(qk_w_in, 16 * 2)
            project(0, range(2 * DT))
            project_v(0, range(QT))
            pe.wait_ge(consts_set, 4)
            pe.wait_ge(consts_in, 16 * N_CONSTS)
            for half in range(2):
                for pair in range(half * H, half * H + H):
                    row_scores(0, pair, behind_turn=pair == H + 2, banks=START_BANKS)
                if half == 1:
                    pe.wait_ge(w_rounded, 1)
                    keep_warm(4, 5)
                turn_max(0, half, (half + 1) * H)
            keep_warm(4, 3)
            for s in range(LAG):
                scores_T(0, s)
                keep_warm(4, 2)
            pe.wait_ge(lost_row_summed, 1)
            nc.tensor.matmul(PS[0:1, 7, 0:1], LOST1[:], ONESF[:], start=True, stop=True).then_inc(lost_all_summed, 1)
            pe.wait_ge(masks_set, 4)
            inexact = []

            def body(b, first, last):
                for s in range(LAG, STEPS):
                    scores_T(b, s)
                    values(b, s - LAG)
                for s in range(STEPS - LAG, STEPS):
                    values(b, s)
                if first:
                    pe.wait_ge(flag_set, 1)
                    inexact.append(pe.value_load(FLAG[0:1, 0:1], min_val=0, max_val=1))
                    pe.wait_ge(w_rounded, len(PIECES))
                if not last:
                    project(b + 1, range(DT))
                else:
                    keep_warm(7, 8)
                turn_x2(b, 0, last)
                if not last:
                    project(b + 1, range(DT, 2 * DT))
                    project_v(b + 1, range(QT - 1))
                else:
                    keep_warm(7, 32)
                turn_x2(b, 1, last)
                if not last:
                    project_v(b + 1, range(QT - 1, QT))
                else:
                    keep_warm(7, 4)
                with pe.If(inexact[0]):
                    feed_forward(b, last, True)
                with pe.Else():
                    feed_forward(b, last, False)

            per_batch(pe, body)


_INS = {
    "x": (B * S, D), "xT": (B * D, S), "wqT": (D, D), "wkT": (D, D), "wvT": (D, D), "bqk": (P, 2 * DT),
    "bv": (D,), "gamma": (D,), "beta": (D,), "w1T": (D, DH), "w2T": (D, DH), "h1T": (DH, DH), "h2T": (DH, DH),
    "scales": (P, 4 * HT), "w3T": (DH, D), "s3": (D,), "ident": (P, P),
}


def kernel(L0_attn_embedded, L0_attn_Wq, L0_attn_bq, L0_attn_Wk, L0_attn_bk, L0_attn_Wv, L0_attn_bv,
           L0_attn_gamma, L0_attn_beta, L0_ffn_w1_w, L0_ffn_w1_s, L0_ffn_w2_w, L0_ffn_w2_s, L0_ffn_h1_w,
           L0_ffn_h1_s, L0_ffn_h2_w, L0_ffn_h2_s, L0_ffn_w3_w, L0_ffn_w3_s):
    import numpy as np
    import concourse.bacc as bacc
    from concourse.bass_utils import run_bass_kernel_spmd

    x = np.asarray(L0_attn_embedded)

    def turned(w):
        return np.ascontiguousarray(np.asarray(w).T)

    def dim_major(w):
        w = np.asarray(w)
        return w.reshape(H, HD, *w.shape[1:]).swapaxes(0, 1).reshape(w.shape)

    def by_partition(*vectors):
        return np.ascontiguousarray(np.concatenate([np.asarray(v).reshape(-1, P) for v in vectors]).T)

    arrays = {
        "x": np.ascontiguousarray(x.reshape(B * S, D)),
        "xT": np.ascontiguousarray(x.transpose(0, 2, 1).reshape(B * D, S)),
        "wqT": turned(dim_major(L0_attn_Wq)), "wkT": turned(dim_major(L0_attn_Wk)), "wvT": turned(L0_attn_Wv),
        "bqk": by_partition(dim_major(L0_attn_bq), dim_major(L0_attn_bk)), "bv": np.asarray(L0_attn_bv),
        "gamma": np.asarray(L0_attn_gamma), "beta": np.asarray(L0_attn_beta),
        "w1T": turned(L0_ffn_w1_w), "w2T": turned(L0_ffn_w2_w),
        "h1T": turned(L0_ffn_h1_w), "h2T": turned(L0_ffn_h2_w), "w3T": turned(L0_ffn_w3_w),
        "scales": by_partition(L0_ffn_w1_s, L0_ffn_w2_s, L0_ffn_h1_s, L0_ffn_h2_s),
        "s3": np.asarray(L0_ffn_w3_s),
        "ident": np.eye(P, dtype=np.float32),
    }
    nc = bacc.Bacc("TRN2", target_bir_lowering=False, num_devices=1,
                   dynamic_dma_scratch_size=1024)
    args = {name: nc.dram_tensor(name + "_dram", shape, F32, kind="ExternalInput").ap()
            for name, shape in _INS.items()}
    args["out"] = nc.dram_tensor("out_dram", (B * S, D), F32, kind="ExternalOutput").ap()
    build_program(nc, **args)
    ran = run_bass_kernel_spmd(nc, [{name + "_dram": arrays[name] for name in _INS}], core_ids=[0])
    return ran.results[0]["out_dram"].reshape(B, S, D)
```
